# Optimizing a Trainium2 kernel written in Bass

```python
import numpy as np
import jax
import jax.numpy as jnp

def _softmax(x, axis=-1):
    return jax.nn.softmax(x, axis=axis)

def _gelu(x):
    return jax.nn.gelu(x, approximate=True)

def _silu(x):
    return jax.nn.silu(x)

def _sigmoid(x):
    return jax.nn.sigmoid(x)

def _layernorm(x, axis=-1, eps=1e-05):
    m = jnp.mean(x, axis=axis, keepdims=True)
    v = jnp.var(x, axis=axis, keepdims=True)
    return (x - m) / jnp.sqrt(v + eps)

def _scatter_add(tgt, idx, src, axis=0):
    return tgt.at[idx].add(src)

def _segment_sum(src, seg, n):
    return jax.ops.segment_sum(src, seg, n)
kernel_name = 'mk_seq_postln_d1_jaxref_r8_b5137a'

def setup_inputs(seed: int=0):
    np.random.seed(seed)
    _w = jnp.asarray

    def _L0_attn_setup():
        import jax, jax.numpy as jnp
        import numpy as np
        C = 256
        A = 256
        HS = 64
        H = A // HS
        DMIX = 32
        DDEC = 64
        B, T = (2, 256)
        EPS = 1e-05 * 8.0 ** 2
        key = jax.random.key(seed)
        ks = jax.random.split(key, 20)
        n = lambda i, shape, s=0.02: jax.random.normal(ks[i], shape, dtype=jnp.float32) * s
        return dict(hidden=jax.random.normal(ks[0], (B, T, C), dtype=jnp.float32), time_maa_x=n(1, (1, 1, C), 0.5), time_maa_w=n(2, (1, 1, C), 0.5), time_maa_k=n(3, (1, 1, C), 0.5), time_maa_v=n(4, (1, 1, C), 0.5), time_maa_r=n(5, (1, 1, C), 0.5), time_maa_g=n(6, (1, 1, C), 0.5), time_maa_w1=n(7, (C, DMIX * 5)), time_maa_w2=n(8, (5, DMIX, C)), time_decay=n(9, (1, 1, A), 0.5), time_decay_w1=n(10, (C, DDEC)), time_decay_w2=n(11, (DDEC, A)), time_faaaa=n(12, (H, HS), 0.5), W_r=n(13, (A, C)), W_k=n(14, (A, C)), W_v=n(15, (A, C)), W_g=n(16, (A, C)), W_o=n(17, (C, A)), ln_gamma=jnp.ones((C,), jnp.float32), ln_beta=jnp.zeros((C,), jnp.float32))
    _L0_attn_in = _L0_attn_setup()

    def _L0_ffn_setup():
        import jax, jax.numpy as jnp
        import numpy as np
        HIDDEN = 256
        INTER = 1024
        SCALE = 64.0

        def fwht(x):
            orig_shape = x.shape
            n = orig_shape[-1]
            x = x.reshape(-1, n)
            h = 1
            while h < n:
                x = x.reshape(-1, n // (2 * h), 2, h)
                a, b = (x[:, :, 0, :], x[:, :, 1, :])
                x = jnp.stack([a + b, a - b], axis=2).reshape(-1, n)
                h *= 2
            return (x / jnp.sqrt(jnp.asarray(n, x.dtype))).reshape(orig_shape)
        key = jax.random.key(seed)
        ks = jax.random.split(key, 8)
        inp = jax.random.normal(ks[0], (4, 256, HIDDEN), dtype=jnp.float32)
        SU_ug = jnp.where(jax.random.bernoulli(ks[1], 0.5, (HIDDEN,)), 1.0, -1.0).astype(jnp.float32)
        SU_dp = jnp.where(jax.random.bernoulli(ks[2], 0.5, (INTER,)), 1.0, -1.0).astype(jnp.float32)
        Wscale_ug = jax.random.uniform(ks[3], (2 * INTER,), jnp.float32, 0.5, 1.5)
        Wscale_dp = jax.random.uniform(ks[4], (HIDDEN,), jnp.float32, 0.5, 1.5)
        W_up = jax.random.normal(ks[5], (INTER, HIDDEN), dtype=jnp.float32) * 0.02
        W_gate = jax.random.normal(ks[6], (INTER, HIDDEN), dtype=jnp.float32) * 0.02
        W_down = jax.random.normal(ks[7], (HIDDEN, INTER), dtype=jnp.float32) * 0.02
        return {'input': inp, 'SU_ug': SU_ug, 'SU_dp': SU_dp, 'Wscale_ug': Wscale_ug, 'Wscale_dp': Wscale_dp, 'W_up': W_up, 'W_gate': W_gate, 'W_down': W_down}
    _L0_ffn_in = _L0_ffn_setup()
    _d = {'L0_attn_hidden': _L0_attn_in['hidden'], 'L0_attn_time_maa_x': _L0_attn_in['time_maa_x'], 'L0_attn_time_maa_w': _L0_attn_in['time_maa_w'], 'L0_attn_time_maa_k': _L0_attn_in['time_maa_k'], 'L0_attn_time_maa_v': _L0_attn_in['time_maa_v'], 'L0_attn_time_maa_r': _L0_attn_in['time_maa_r'], 'L0_attn_time_maa_g': _L0_attn_in['time_maa_g'], 'L0_attn_time_maa_w1': _L0_attn_in['time_maa_w1'], 'L0_attn_time_maa_w2': _L0_attn_in['time_maa_w2'], 'L0_attn_time_decay': _L0_attn_in['time_decay'], 'L0_attn_time_decay_w1': _L0_attn_in['time_decay_w1'], 'L0_attn_time_decay_w2': _L0_attn_in['time_decay_w2'], 'L0_attn_time_faaaa': _L0_attn_in['time_faaaa'], 'L0_attn_W_r': _L0_attn_in['W_r'], 'L0_attn_W_k': _L0_attn_in['W_k'], 'L0_attn_W_v': _L0_attn_in['W_v'], 'L0_attn_W_g': _L0_attn_in['W_g'], 'L0_attn_W_o': _L0_attn_in['W_o'], 'L0_attn_ln_gamma': _L0_attn_in['ln_gamma'], 'L0_attn_ln_beta': _L0_attn_in['ln_beta'], 'L0_ffn_SU_ug': _L0_ffn_in['SU_ug'], 'L0_ffn_SU_dp': _L0_ffn_in['SU_dp'], 'L0_ffn_Wscale_ug': _L0_ffn_in['Wscale_ug'], 'L0_ffn_Wscale_dp': _L0_ffn_in['Wscale_dp'], 'L0_ffn_W_up': _L0_ffn_in['W_up'], 'L0_ffn_W_gate': _L0_ffn_in['W_gate'], 'L0_ffn_W_down': _L0_ffn_in['W_down']}
    _x0 = _d['L0_attn_hidden']
    _d['L0_attn_hidden'] = jax.random.normal(jax.random.fold_in(jax.random.key(seed), 1), (1, 1024, 256), dtype=_x0.dtype)
    del _x0
    return _d

def reference(L0_attn_hidden, L0_attn_time_maa_x, L0_attn_time_maa_w, L0_attn_time_maa_k, L0_attn_time_maa_v, L0_attn_time_maa_r, L0_attn_time_maa_g, L0_attn_time_maa_w1, L0_attn_time_maa_w2, L0_attn_time_decay, L0_attn_time_decay_w1, L0_attn_time_decay_w2, L0_attn_time_faaaa, L0_attn_W_r, L0_attn_W_k, L0_attn_W_v, L0_attn_W_g, L0_attn_W_o, L0_attn_ln_gamma, L0_attn_ln_beta, L0_ffn_SU_ug, L0_ffn_SU_dp, L0_ffn_Wscale_ug, L0_ffn_Wscale_dp, L0_ffn_W_up, L0_ffn_W_gate, L0_ffn_W_down):

    def _L0_attn_ref(hidden, time_maa_x, time_maa_w, time_maa_k, time_maa_v, time_maa_r, time_maa_g, time_maa_w1, time_maa_w2, time_decay, time_decay_w1, time_decay_w2, time_faaaa, W_r, W_k, W_v, W_g, W_o, ln_gamma, ln_beta):
        import jax, jax.numpy as jnp
        import numpy as np
        C = 256
        A = 256
        HS = 64
        H = A // HS
        DMIX = 32
        DDEC = 64
        B, T = (2, 256)
        EPS = 1e-05 * 8.0 ** 2
        Bq, Tq, Cq = hidden.shape
        shifted = jnp.pad(hidden, ((0, 0), (1, 0), (0, 0)))[:, :-1]
        xx = shifted - hidden
        xxx = hidden + xx * time_maa_x
        z = jnp.tanh(jnp.einsum('btc,cd->btd', xxx, time_maa_w1)).reshape(Bq, Tq, 5, DMIX)
        mix = jnp.einsum('btfd,fdc->fbtc', z, time_maa_w2)
        mw, mk, mv, mr, mg = (mix[0], mix[1], mix[2], mix[3], mix[4])
        xw = hidden + xx * (time_maa_w + mw)
        xk = hidden + xx * (time_maa_k + mk)
        xv = hidden + xx * (time_maa_v + mv)
        xr = hidden + xx * (time_maa_r + mr)
        xg = hidden + xx * (time_maa_g + mg)
        r = jnp.einsum('btc,ac->bta', xr, W_r)
        k = jnp.einsum('btc,ac->bta', xk, W_k)
        v = jnp.einsum('btc,ac->bta', xv, W_v)
        g = jax.nn.silu(jnp.einsum('btc,ac->bta', xg, W_g))
        dd = jnp.einsum('btd,da->bta', jnp.tanh(jnp.einsum('btc,cd->btd', xw, time_decay_w1)), time_decay_w2) + time_decay
        w = jnp.exp(-jnp.exp(dd))
        rh = r.reshape(Bq, Tq, H, HS).transpose(1, 0, 2, 3)
        kh = k.reshape(Bq, Tq, H, HS).transpose(1, 0, 2, 3)
        vh = v.reshape(Bq, Tq, H, HS).transpose(1, 0, 2, 3)
        wh = w.reshape(Bq, Tq, H, HS).transpose(1, 0, 2, 3)
        u = time_faaaa

        def step(S, inputs):
            r_t, k_t, v_t, w_t = inputs
            kv = k_t[..., :, None] * v_t[..., None, :]
            out_t = jnp.einsum('bhn,bhnm->bhm', r_t, u[None, :, :, None] * kv + S)
            S = kv + w_t[..., :, None] * S
            return (S, out_t)
        S0 = jnp.zeros((Bq, H, HS, HS), dtype=hidden.dtype)
        _, outs = jax.lax.scan(step, S0, (rh, kh, vh, wh))
        out = outs.transpose(1, 0, 2, 3)
        mean = out.mean(-1, keepdims=True)
        var = out.var(-1, keepdims=True)
        out = (out - mean) * jax.lax.rsqrt(var + EPS)
        out = out.reshape(Bq, Tq, Cq) * ln_gamma + ln_beta
        out = out * g
        return jnp.einsum('bta,ca->btc', out, W_o)

    def _L0_ffn_ref(input, SU_ug, SU_dp, Wscale_ug, Wscale_dp, W_up, W_gate, W_down):
        import jax, jax.numpy as jnp
        import numpy as np
        HIDDEN = 256
        INTER = 1024
        SCALE = 64.0

        def fwht(x):
            orig_shape = x.shape
            n = orig_shape[-1]
            x = x.reshape(-1, n)
            h = 1
            while h < n:
                x = x.reshape(-1, n // (2 * h), 2, h)
                a, b = (x[:, :, 0, :], x[:, :, 1, :])
                x = jnp.stack([a + b, a - b], axis=2).reshape(-1, n)
                h *= 2
            return (x / jnp.sqrt(jnp.asarray(n, x.dtype))).reshape(orig_shape)
        n = SU_ug.shape[0]
        x = input.reshape(-1, n)
        x = fwht(x * SU_ug) / SCALE
        x_up = x @ W_up.T * (Wscale_ug[:INTER] * SCALE)
        x_gate = x @ W_gate.T * (Wscale_ug[INTER:] * SCALE)
        x = jax.nn.silu(x_gate) * x_up
        x = fwht(x * SU_dp) / SCALE
        x = x @ W_down.T * (Wscale_dp * SCALE)
        return x.reshape(input.shape)
    x = L0_attn_hidden
    x = _layernorm(x + _L0_attn_ref(x, L0_attn_time_maa_x, L0_attn_time_maa_w, L0_attn_time_maa_k, L0_attn_time_maa_v, L0_attn_time_maa_r, L0_attn_time_maa_g, L0_attn_time_maa_w1, L0_attn_time_maa_w2, L0_attn_time_decay, L0_attn_time_decay_w1, L0_attn_time_decay_w2, L0_attn_time_faaaa, L0_attn_W_r, L0_attn_W_k, L0_attn_W_v, L0_attn_W_g, L0_attn_W_o, L0_attn_ln_gamma, L0_attn_ln_beta), axis=-1)
    x = _layernorm(x + _L0_ffn_ref(x, L0_ffn_SU_ug, L0_ffn_SU_dp, L0_ffn_Wscale_ug, L0_ffn_Wscale_dp, L0_ffn_W_up, L0_ffn_W_gate, L0_ffn_W_down), axis=-1)
    return x

_drawn_inputs = setup_inputs


def setup_inputs(seed=0):
    import zlib

    import numpy as np

    out = dict(_drawn_inputs(seed))
    spreads = {'L0_attn_ln_gamma': (1.0, 0.6), 'L0_attn_ln_beta': (0.0, 0.8)}
    factors = {'L0_attn_time_maa_x': 8.0,
     'L0_attn_time_maa_w': 8.0,
     'L0_attn_time_maa_w1': 7.769,
     'L0_attn_time_maa_w2': 7.753,
     'L0_attn_time_decay': 2.755,
     'L0_attn_time_decay_w1': 8.0,
     'L0_attn_time_decay_w2': 8.0,
     'L0_ffn_Wscale_ug': 3.98,
     'L0_ffn_Wscale_dp': 5.539}
    for name, (base, spread) in spreads.items():
        noise = np.random.default_rng([zlib.crc32(name.encode()), seed]).standard_normal(out[name].shape)
        drawn = base * np.exp(spread * noise) if base else spread * noise
        out[name] = jnp.asarray(drawn.astype(out[name].dtype))
    for name, factor in factors.items():
        out[name] = (out[name] * factor).astype(out[name].dtype)
    return out
```

```python
from contextlib import ExitStack

import concourse.bass as bass
from concourse import mybir

F32 = mybir.dt.float32
U32 = mybir.dt.uint32
ACT = mybir.ActivationFunctionType
ALU = mybir.AluOpType

T = 1024
C = 256
P = 128
CH = C // P
HS = 64
HEADS = C // HS
TG = 256
G = T // TG
Q = 128
J = TG // Q
DMIX = 32
DDEC = 64
INTER = 1024
IT = INTER // P
LEVELS = [1, 2, 4, 8, 16, 32, 64]
HALF = Q // 2
FFN_SCALE = 64.0
GN_EPS = 1e-05 * 8.0 ** 2
LN_EPS = 1e-05

VEC = {}
_at = 0
for _name, _n in [("maa_x", CH), ("maa_w", CH), ("maa_k", CH), ("maa_r", CH), ("maa_v", CH), ("maa_g", CH),
                  ("decay", CH), ("u", CH), ("gamma", CH), ("beta", CH), ("su_ug", CH), ("ws_up", IT),
                  ("ws_gate", IT), ("su_dp", IT)]:
    VEC[_name] = _at
    _at += _n
VCOLS = _at

PART = {"w": 0, "k": 1, "v": 2, "r": 3, "g": 4}
MIXES = ["w", "k", "r", "v", "g"]
MIX_BANK = {"w": 1, "k": 2, "r": 3, "v": 4, "g": 0}
LEVEL_BANKS = [(4, 0), (2, 3)]
DIAG_BANKS = (2, 3)
OUT_BANK = [2, 4]
STATE_BANK = [3, 0]
UG_BANK = [5, 6]
FFN_BANK = 7


def wait_last(eng, sem, value):
    if not isinstance(value, int) or value > 0:
        eng.wait_ge(sem, value)


def build(nc, d):
    with ExitStack() as ctx:
        def sb(name, shape, dt=F32):
            return ctx.enter_context(nc.sbuf_tensor(name, shape, dt))

        def sem(name):
            return ctx.enter_context(nc.semaphore(name))

        def moment_tiles(name, n):
            return {k: sb(f"{name}_{k}", [P, n]) for k in ("sum", "diff", "m2", "sq", "mean", "var", "m2n")}

        bank = [ctx.enter_context(nc.psum_tensor(f"bank{i}", [P, 512], F32)) for i in range(8)]

        xT = sb("xT", [P, CH, TG + 1])
        xtok = sb("xtok", [P, J, C])
        vec = sb("vec", [P, VCOLS])
        w1 = sb("w1", [P, CH, 5 * DMIX])
        w2 = sb("w2", [P, C])
        w2g = sb("w2g", [DMIX, C])
        dw1 = sb("dw1", [P, CH, DDEC])
        dw2 = sb("dw2", [DDEC, C])
        proj = {n: sb(f"W_{n}", [P, CH, C]) for n in "krvgo"}
        wup = sb("wup", [P, CH, INTER])
        wgate = sb("wgate", [P, CH, INTER])
        wdown = sb("wdown", [P, IT, C])
        wd_tmp = sb("wd_tmp", [P, IT, C])
        wsrow = sb("wsrow", [P, C])
        had = sb("had", [P, P])
        ident = sb("ident", [P, P])
        masks = sb("masks", [P, Q + HALF * len(LEVELS)])
        neghalf = sb("neghalf", [P, J * HEADS])

        xx = sb("xx", [P, CH, TG])
        xxx = sb("xxx", [P, CH, TG])
        mixed = sb("mixed", [P, 2, CH, TG])
        xm = {n: sb(f"x_{n}", [P, CH, TG]) for n in MIXES}
        zt = sb("zt", [P, TG])
        ztg = sb("ztg", [DMIX, TG])
        tdec = sb("tdec", [DDEC, TG])
        edec = sb("edec", [P, CH, TG])
        wdec = [sb(f"wdec{L}", [P, CH, TG // L]) for L in LEVELS + [Q]]
        kq = sb("kq", [P, CH, TG])
        rq = sb("rq", [P, CH, TG])
        uk = sb("uk", [P, CH, TG])
        vs = sb("vs", [P, J, C])
        gT = sb("gT", [P, CH, TG])
        A = [sb(f"A{e}", [P, J, CH, Q]) for e in range(2)]
        kT = sb("kT", [P, J, CH, P])
        S = sb("S", [P, CH, P])
        gstat = sb("gstat", [P, J * HEADS, 6])
        gm = moment_tiles("gm", J * HEADS)
        grs = sb("grs", [P, J * HEADS])
        norm = sb("norm", [P, J, C])
        nT = sb("nT", [P, CH, TG])
        og = sb("og", [P, CH, TG])
        res = sb("res", [P, J, C])
        stat1 = sb("stat1", [P, J, 6])
        m1 = moment_tiles("m1", J)
        rs1 = sb("rs1", [P, J])
        y = sb("y", [P, J, C])

        wsu = sb("wsu", [P, 2 * IT])
        sdu = sb("sdu", [P, IT])
        ya = sb("ya", [P, TG])
        yu = sb("yu", [P, CH, TG])
        xh = sb("xh", [P, CH, TG])
        sg = sb("sg", [P, 2, TG])
        h = sb("h", [P, IT, TG])
        res2 = sb("res2", [P, J, C])
        stat2 = sb("stat2", [P, J, 6])
        m2 = moment_tiles("m2", J)
        rs2 = sb("rs2", [P, J])
        outs = sb("outs", [P, J, C])

        L = {n: sem(f"load_{n}") for n in ( "vec", "w1", "w2", "dw", "W_k", "W_r", "W_v", "W_g",
                                           "W_o", "wug", "wdown", "wsrow", "const", "masks")}
        zeroed = sem("zeroed")
        xT_loaded = sem("xT_loaded")
        xtok_loaded = sem("xtok_loaded")
        xxx_ready = sem("xxx_ready")
        z_psum = sem("z_psum")
        z_tanh = sem("z_tanh")
        mix_psum = sem("mix_psum")
        mixed_ready = sem("mixed_ready")
        xm_ready = sem("xm_ready")
        dec1_psum = sem("dec1_psum")
        dec1_tanh = sem("dec1_tanh")
        dec2_psum = sem("dec2_psum")
        exp_ready = sem("exp_ready")
        w_ready = sem("w_ready")
        k_psum = sem("k_psum")
        r_psum = sem("r_psum")
        v_psum = sem("v_psum")
        g_psum = sem("g_psum")
        k_ready = sem("k_ready")
        r_ready = sem("r_ready")
        v_ready = sem("v_ready")
        g_ready = sem("g_ready")
        level_psum = sem("level_psum")
        q_scaled = sem("q_scaled")
        k_scaled = sem("k_scaled")
        wprod = sem("wprod")
        diag_copied = sem("diag_copied")
        A_copied = sem("A_copied")
        kT_psum = sem("kT_psum")
        kT_ready = sem("kT_ready")
        o_psum = sem("o_psum")
        st_psum = sem("st_psum")
        S_ready = sem("S_ready")
        gvar_ready = sem("gvar_ready")
        grs_ready = sem("grs_ready")
        norm_ready = sem("norm_ready")
        nT_psum = sem("nT_psum")
        nT_ready = sem("nT_ready")
        og_ready = sem("og_ready")
        wo_psum = sem("wo_psum")
        res_ready = sem("res_ready")
        var1_ready = sem("var1_ready")
        rs1_ready = sem("rs1_ready")
        y_ready = sem("y_ready")
        scales_ready = sem("scales_ready")
        wd_step = sem("wd_step")
        wd_psum = sem("wd_psum")
        wd_ready = sem("wd_ready")
        yT_psum = sem("yT_psum")
        ya_ready = sem("ya_ready")
        yu_ready = sem("yu_ready")
        xh_psum = sem("xh_psum")
        xh_ready = sem("xh_ready")
        ug_psum = sem("ug_psum")
        silu_ready = sem("silu_ready")
        h_ready = sem("h_ready")
        dn_psum = sem("dn_psum")
        res2_ready = sem("res2_ready")
        var2_ready = sem("var2_ready")
        rs2_ready = sem("rs2_ready")
        out_ready = sem("out_ready")
        stored = sem("stored")
        xx_done = sem("xx_done")
        gstat_done = sem("gstat_done")
        gmv_done = sem("gmv_done")
        stat1_done = sem("stat1_done")
        mv1_done = sem("mv1_done")
        stat2_done = sem("stat2_done")
        mv2_done = sem("mv2_done")

        def vcol(name, i, lo=0, hi=P):
            return vec[lo:hi, VEC[name] + i:VEC[name] + i + 1]

        now, before = xT[:, :, 1:TG + 1], xT[:, :, 0:TG]

        def flat(t):
            return t[:].rearrange("p c t -> p (c t)")

        def half(b, c):
            return bank[b][:, c * TG:(c + 1) * TG]

        def halves(b):
            return bank[b][:, :].rearrange("p (c t) -> p c t", c=2)

        block = ctx.enter_context(nc.Block())

        @block.sync
        def _(sp):
            sp.dma_start(now, d["xT"][:, :, 0:TG]).then_inc(xT_loaded, 16)
            sp.dma_start(w1[:], d["w1"]).then_inc(L["w1"], 16)
            sp.dma_start(dw1[:], d["dw1"]).then_inc(L["dw"], 16)
            sp.dma_start(proj["k"][:], d["W_k"]).then_inc(L["W_k"], 16)
            sp.dma_start(proj["r"][:], d["W_r"]).then_inc(L["W_r"], 16)
            sp.dma_start(masks[:], d["masks"]).then_inc(L["masks"], 16)
            sp.dma_start(xtok[:], d["xtok"][:, 0:J, :]).then_inc(xtok_loaded, 16)
            sp.dma_start(wup[:], d["wup"]).then_inc(L["wug"], 16)

            def load_xT(g):
                wait_last(sp, xm_ready, 5 * g)
                sp.dma_start(xT[:], d["xT"][:, :, bass.ds(g * TG - 1, TG + 1)]).then_inc(xT_loaded, 16)

            def load_xtok(g):
                wait_last(sp, res_ready, g)
                sp.dma_start(xtok[:], d["xtok"][:, bass.ds(g * J, J), :]).then_inc(xtok_loaded, 16)

            def store(g):
                sp.wait_ge(out_ready, g + 1)
                sp.dma_start(d["out"][:, bass.ds(g * J, J), :], outs[:]).then_inc(stored, 16)

            load_xT(1)
            load_xtok(1)
            with sp.Fori(1, G - 1) as g:
                load_xT(g + 1)
                store(g - 1)
                load_xtok(g + 1)
            store(G - 2)
            store(G - 1)
            sp.wait_ge(stored, 16 * G)

        @block.gpsimd
        def _(pool):
            nc.gpsimd.memset(xT[:, :, 0:1], 0.0)
            nc.gpsimd.memset(neghalf[:], -0.5)
            nc.gpsimd.memset(S[:], 0.0)
            nc.gpsimd.memset(A[0][:], 0.0)
            nc.gpsimd.memset(A[1][:], 0.0).then_inc(zeroed, 1)
            pool.wait_ge(zeroed, 1)

            def mix_add(g, i):
                pool.wait_ge(mixed_ready, 5 * g + i + 1)
                wait_last(pool, {"w": dec1_psum, "k": k_psum, "r": r_psum, "v": v_psum, "g": g_psum}[MIXES[i]], g)
                nc.gpsimd.tensor_tensor(xm[MIXES[i]][:], mixed[:, i % 2], now, ALU.add).then_inc(xm_ready, 1)

            def scale_k(g, n):
                Ln = LEVELS[n]
                pool.wait_ge(level_psum, 7 * g + n + 1)
                if n == 0:
                    pool.wait_ge(w_ready, g + 1)
                else:
                    pool.wait_ge(wprod, 7 * g + n)
                    pool.wait_ge(k_scaled, 7 * g + n)
                kk = kq[:].rearrange("p c (b e l) -> p (c b) e l", e=2, l=Ln)[:, :, 0]
                ww = wdec[n][:].rearrange("p c (b e) -> p (c b) e", e=2)[:, :, 1:2].to_broadcast([P, CH * TG // (2 * Ln), Ln])
                nc.gpsimd.tensor_tensor(kk, kk, ww, ALU.mult).then_inc(k_scaled, 1)

            def group_rsqrt(g):
                pool.wait_ge(gvar_ready, g + 1)
                wait_last(pool, norm_ready, g)
                nc.gpsimd.tensor_tensor(grs[:], gm["var"][:], neghalf[:], ALU.pow).then_inc(grs_ready, 1)

            def gate(g):
                pool.wait_ge(nT_ready, g + 1)
                pool.wait_ge(g_ready, g + 1)
                wait_last(pool, wo_psum, g)
                nc.gpsimd.tensor_tensor(og[:], nT[:], gT[:], ALU.mult).then_inc(og_ready, 1)

            def rsqrt1(g):
                pool.wait_ge(var1_ready, g + 1)
                wait_last(pool, y_ready, g)
                nc.gpsimd.tensor_tensor(rs1[:], m1["var"][:], neghalf[:, 0:J], ALU.pow).then_inc(rs1_ready, 1)

            def rsqrt2(g):
                pool.wait_ge(var2_ready, g + 1)
                wait_last(pool, out_ready, g)
                nc.gpsimd.tensor_tensor(rs2[:], m2["var"][:], neghalf[:, 0:J], ALU.pow).then_inc(rs2_ready, 1)

            def mixing(g, ffn=None):
                for i in range(5):
                    mix_add(g, i)
                for n in range(7):
                    scale_k(g, n)
                group_rsqrt(g)
                gate(g)
                if ffn is not None:
                    rsqrt2(ffn)
                rsqrt1(g)

            mixing(0)
            mixing(1, 0)
            with pool.Fori(2, G) as g:
                mixing(g, g - 1)
            rsqrt2(G - 1)

        @block.scalar
        def _(act):
            act.dma_start(vec[:], d["vec"]).then_inc(L["vec"], 16)
            act.dma_start(w2[:], d["w2"]).then_inc(L["w2"], 16)
            act.dma_start(w2g[:], d["w2g"]).then_inc(L["w2"], 16)
            act.dma_start(dw2[:], d["dw2"]).then_inc(L["dw"], 16)
            act.dma_start(proj["v"][:], d["W_v"]).then_inc(L["W_v"], 16)
            act.dma_start(proj["g"][:], d["W_g"]).then_inc(L["W_g"], 16)
            act.dma_start(had[:], d["had"]).then_inc(L["const"], 16)
            act.dma_start(ident[:], d["ident"]).then_inc(L["const"], 16)
            act.dma_start(wdown[:], d["wdown"]).then_inc(L["wdown"], 16)
            act.dma_start(wsrow[:], d["wsrow"].to_broadcast([P, C])).then_inc(L["wsrow"], 16)
            act.dma_start(proj["o"][:], d["W_o"]).then_inc(L["W_o"], 16)
            act.dma_start(wgate[:], d["wgate"]).then_inc(L["wug"], 16)

            def z(g):
                act.wait_ge(z_psum, g + 1)
                wait_last(act, mix_psum, 5 * g)
                nc.scalar.activation(zt[:], half(0, 0), ACT.Tanh)
                nc.scalar.activation(ztg[:], bank[0][0:DMIX, TG:2 * TG], ACT.Tanh).then_inc(z_tanh, 1)

            def decay_tanh(g):
                act.wait_ge(dec1_psum, g + 1)
                wait_last(act, dec2_psum, g)
                nc.scalar.activation(tdec[:], bank[1][0:DDEC, 0:TG], ACT.Tanh).then_inc(dec1_tanh, 1)

            def k_out(g):
                act.wait_ge(k_psum, g + 1)
                wait_last(act, kT_psum, g)
                wait_last(act, k_scaled, 7 * g)
                nc.scalar.copy(kq[:], halves(2))
                for c in range(CH):
                    last = nc.scalar.activation(uk[:, c], half(2, c), ACT.Copy, scale=vcol("u", c))
                last.then_inc(k_ready, 1)

            def decay(g):
                act.wait_ge(dec2_psum, g + 1)
                wait_last(act, w_ready, g)
                for c in range(CH):
                    last = nc.scalar.activation(edec[:, c], half(3, c), ACT.Exp, bias=vcol("decay", c))
                last.then_inc(exp_ready, 1)
                act.wait_ge(exp_ready, g + 1)
                wait_last(act, wprod, 7 * g)
                wait_last(act, k_scaled, 7 * g)
                nc.scalar.activation(wdec[0][:], edec[:], ACT.Exp, scale=-1.0).then_inc(w_ready, 1)

            def r_out(g):
                act.wait_ge(r_psum, g + 1)
                wait_last(act, q_scaled, 7 * g)
                wait_last(act, o_psum, 2 * g)
                nc.scalar.copy(rq[:], halves(4)).then_inc(r_ready, 1)

            def v_out(g):
                act.wait_ge(v_psum, g + 1)
                wait_last(act, st_psum, 2 * g)
                nc.scalar.copy(vs[:], halves(0)).then_inc(v_ready, 1)

            def g_out(g):
                act.wait_ge(g_psum, g + 1)
                wait_last(act, og_ready, g)
                nc.scalar.activation(gT[:], halves(1), ACT.Silu).then_inc(g_ready, 1)

            def kT_out(g):
                act.wait_ge(kT_psum, g + 1)
                wait_last(act, st_psum, 2 * g)
                nc.scalar.copy(kT[:], bank[1][:].rearrange("p (j c n) -> p j c n", j=J, c=CH)).then_inc(kT_ready, 1)

            def affine(g):
                act.wait_ge(nT_psum, g + 1)
                wait_last(act, og_ready, g)
                for c in range(CH):
                    last = nc.scalar.activation(nT[:, c], half(1, c), ACT.Identity, bias=vcol("beta", c),
                                                scale=vcol("gamma", c))
                last.then_inc(nT_ready, 1)

            def y_signed(g):
                act.wait_ge(yT_psum, g + 1)
                wait_last(act, yu_ready, g)
                nc.scalar.activation(ya[:], half(FFN_BANK, 0), ACT.Copy, scale=vcol("su_ug", 0)).then_inc(ya_ready, 1)

            def x_rotated(g):
                act.wait_ge(xh_psum, g + 1)
                wait_last(act, ug_psum, 8 * g)
                s = 1.0 / (C ** 0.5 * FFN_SCALE)
                nc.scalar.mul(xh[:, 0], half(FFN_BANK, 0), s)
                nc.scalar.mul(xh[:, 1], half(FFN_BANK, 1), -s).then_inc(xh_ready, 1)

            def silu(g, it):
                act.wait_ge(ug_psum, 8 * g + it + 1)
                wait_last(act, h_ready, 8 * g + max(it - 1, 0))
                nc.scalar.activation(sg[:, it % 2], half(UG_BANK[it % 2], 1), ACT.Silu,
                                     scale=wsu[:, IT + it:IT + it + 1]).then_inc(silu_ready, 1)

            def group(g, f=None):
                z(g)
                if f is not None:
                    y_signed(f)
                    x_rotated(f)
                decay_tanh(g)
                k_out(g)
                decay(g)
                r_out(g)
                v_out(g)
                g_out(g)
                if f is not None:
                    for it in range(IT):
                        silu(f, it)
                kT_out(g)
                affine(g)

            act.wait_ge(L["vec"], 16)
            group(0)
            act.wait_ge(scales_ready, 1)
            group(1, 0)
            with act.Fori(2, G) as g:
                group(g, g - 1)
            y_signed(G - 1)
            x_rotated(G - 1)
            for it in range(IT):
                silu(G - 1, it)

        @block.vector
        def _(dve):
            def token_mix(g):
                dve.wait_ge(xT_loaded, 16 * g + 16)
                nc.vector.tensor_tensor(xx[:], before, now, ALU.subtract).then_inc(xx_done, 1)
                dve.wait_ge(xx_done, g + 1)
                wait_last(dve, z_psum, g)
                for c in range(CH):
                    last = nc.vector.scalar_tensor_tensor(xxx[:, c], xx[:, c], vcol("maa_x", c), now[:, c],
                                                          ALU.mult, ALU.add)
                last.then_inc(xxx_ready, 1)

            def mix(g, i):
                dve.wait_ge(mix_psum, 5 * g + i + 1)
                wait_last(dve, xm_ready, 5 * g + max(i - 1, 0))
                for c in range(CH):
                    last = nc.vector.scalar_tensor_tensor(mixed[:, i % 2, c], half(MIX_BANK[MIXES[i]], c),
                                                          vcol("maa_" + MIXES[i], c), xx[:, c], ALU.add, ALU.mult)
                last.then_inc(mixed_ready, 1)

            def level(g, n):
                Ln = LEVELS[n]
                nb = TG // (2 * Ln)
                dve.wait_ge(level_psum, 7 * g + n + 1)
                if n == 0:
                    dve.wait_ge(w_ready, g + 1)
                else:
                    dve.wait_ge(wprod, 7 * g + n)
                    dve.wait_ge(q_scaled, 7 * g + n)
                qq = rq[:].rearrange("p c (b e l) -> p (c b) e l", e=2, l=Ln)[:, :, 1]
                w4 = wdec[n][:].rearrange("p c (b e) -> p (c b) e", e=2)
                nc.vector.tensor_tensor(qq, qq, w4[:, :, 0:1].to_broadcast([P, CH * nb, Ln]),
                                        ALU.mult).then_inc(q_scaled, 1)
                if n == 0:
                    for e in range(2):
                        last = nc.vector.copy_predicated(
                            A[e][:].rearrange("p j c t -> p (j c) t"),
                            masks[:, 0:Q].bitcast(U32).rearrange("p (a t) -> p a t", a=1).to_broadcast([P, J * CH, Q]),
                            bank[DIAG_BANKS[e]][:].rearrange("p (a t) -> p a t", a=J * CH))
                    last.then_inc(diag_copied, 1)
                    dve.wait_ge(diag_copied, g + 1)
                else:
                    dve.wait_ge(A_copied, 7 * g + n)
                nc.vector.tensor_tensor(wdec[n + 1][:].rearrange("p c b -> p (c b)"), w4[:, :, 0], w4[:, :, 1],
                                        ALU.mult).then_inc(wprod, 1)
                m0 = Q + HALF * n
                for e in range(2):
                    nbq = Q // (2 * Ln)
                    last = nc.vector.copy_predicated(
                        A[e][:].rearrange("p j c (b e l) -> p (j c) b e l", e=2, l=Ln)[:, :, :, 1],
                        masks[:, m0:m0 + HALF].bitcast(U32).rearrange("p (a b l) -> p a b l", a=1, l=Ln).to_broadcast(
                            [P, J * CH, nbq, Ln]),
                        bank[LEVEL_BANKS[n % 2][e]][:, 0:J * CH * HALF].rearrange("p (a b l) -> p a b l", a=J * CH,
                                                                                  l=Ln))
                last.then_inc(A_copied, 1)

            def state(g, j):
                dve.wait_ge(st_psum, 2 * g + j + 1)
                dve.wait_ge(o_psum, 2 * g + j + 1)
                wait_last(dve, S_ready, 2 * g + j)
                dve.wait_ge(wprod, 7 * g + 7)
                for c in range(CH):
                    for e in range(2):
                        lo, hi = e * HS, (e + 1) * HS
                        last = nc.vector.scalar_tensor_tensor(
                            S[lo:hi, c, lo:hi], S[lo:hi, c, lo:hi], wdec[7][lo:hi, c, j:j + 1],
                            bank[STATE_BANK[j]][lo:hi, c * P + lo:c * P + hi], ALU.mult, ALU.add)
                last.then_inc(S_ready, 1)

            def moments(g, stat, m, n, eps, parts_done, var_ready):
                nc.vector.tensor_tensor(m["sum"][:], stat[:, :, 1], stat[:, :, 4], ALU.add)
                nc.vector.tensor_tensor(m["diff"][:], stat[:, :, 1], stat[:, :, 4], ALU.subtract)
                nc.vector.tensor_tensor(m["m2"][:], stat[:, :, 2], stat[:, :, 5], ALU.add).then_inc(parts_done, 1)
                dve.wait_ge(parts_done, 2 * g + 1)
                nc.vector.tensor_scalar(m["mean"][:], m["sum"][:], 0.5, None, ALU.mult)
                nc.vector.scalar_tensor_tensor(m["sq"][:], m["diff"][:], 0.25, m["diff"][:], ALU.mult, ALU.mult)
                nc.vector.tensor_scalar(m["m2n"][:], m["m2"][:], 1.0 / n, eps, ALU.mult,
                                        ALU.add).then_inc(parts_done, 1)
                dve.wait_ge(parts_done, 2 * g + 2)
                nc.vector.tensor_tensor(m["var"][:], m["sq"][:], m["m2n"][:], ALU.add).then_inc(var_ready, 1)

            def group_norm(g):
                for j in range(J):
                    dve.wait_ge(o_psum, 2 * g + j + 1)
                    for hh in range(HEADS):
                        last = nc.vector.bn_stats(gstat[:, j * HEADS + hh],
                                                  bank[OUT_BANK[j]][:, hh * HS:(hh + 1) * HS])
                last.then_inc(gstat_done, 1)
                dve.wait_ge(gstat_done, g + 1)
                wait_last(dve, grs_ready, g)
                moments(g, gstat, gm, HS, GN_EPS, gmv_done, gvar_ready)
                dve.wait_ge(grs_ready, g + 1)
                wait_last(dve, nT_psum, g)
                for a in range(J * HEADS):
                    j, hh = divmod(a, HEADS)
                    last = nc.vector.tensor_scalar(norm[:, j, hh * HS:(hh + 1) * HS],
                                                   bank[OUT_BANK[j]][:, hh * HS:(hh + 1) * HS], gm["mean"][:, a:a + 1],
                                                   grs[:, a:a + 1], ALU.subtract, ALU.mult)
                last.then_inc(norm_ready, 1)

            def residual1(g):
                dve.wait_ge(wo_psum, g + 1)
                wait_last(dve, y_ready, g)
                dve.wait_ge(xtok_loaded, 16 * g + 16)
                nc.vector.tensor_tensor(res[:], halves(3), xtok[:], ALU.add).then_inc(res_ready, 1)
                dve.wait_ge(res_ready, g + 1)
                for j in range(J):
                    last = nc.vector.bn_stats(stat1[:, j], res[:, j])
                last.then_inc(stat1_done, 1)
                dve.wait_ge(stat1_done, g + 1)
                moments(g, stat1, m1, C, LN_EPS, mv1_done, var1_ready)

            def norm1(g):
                dve.wait_ge(rs1_ready, g + 1)
                wait_last(dve, yT_psum, g)
                wait_last(dve, res2_ready, g)
                for j in range(J):
                    last = nc.vector.tensor_scalar(y[:, j], res[:, j], m1["mean"][:, j:j + 1], rs1[:, j:j + 1], ALU.subtract,
                                                   ALU.mult)
                last.then_inc(y_ready, 1)

            def rotate_down():
                dve.wait_ge(L["wdown"], 16)
                bufs = [wdown, wd_tmp, wdown, wd_tmp]
                for s, dist in enumerate((4, 2, 1)):
                    a = bufs[s][:].rearrange("p (b e l) c -> p b e (l c)", e=2, l=dist)
                    o = bufs[s + 1][:].rearrange("p (b e l) c -> p b e (l c)", e=2, l=dist)
                    if s:
                        dve.wait_ge(wd_step, s)
                    nc.vector.tensor_tensor(o[:, :, 0], a[:, :, 0], a[:, :, 1], ALU.add)
                    nc.vector.tensor_tensor(o[:, :, 1], a[:, :, 0], a[:, :, 1], ALU.subtract).then_inc(wd_step, 1)

            def scale_down():
                dve.wait_ge(L["wsrow"], 16)
                for i in range(IT // 2):
                    dve.wait_ge(wd_psum, i + 1)
                    for e in range(2):
                        it = 2 * i + e
                        last = nc.vector.scalar_tensor_tensor(wdown[:, it], half(UG_BANK[i % 2], e), sdu[:, it:it + 1],
                                                              wsrow[:], ALU.mult, ALU.mult)
                    last.then_inc(wd_ready, 1)

            def y_butterfly(g):
                dve.wait_ge(ya_ready, g + 1)
                wait_last(dve, xh_psum, g)
                nc.vector.scalar_tensor_tensor(yu[:, 0], half(FFN_BANK, 1), vcol("su_ug", 1), ya[:], ALU.mult, ALU.add)
                nc.vector.scalar_tensor_tensor(yu[:, 1], half(FFN_BANK, 1), vcol("su_ug", 1), ya[:], ALU.mult,
                                               ALU.subtract).then_inc(yu_ready, 1)

            def swiglu(g, it):
                dve.wait_ge(silu_ready, 8 * g + it + 1)
                if it == 0:
                    wait_last(dve, dn_psum, g)
                nc.vector.scalar_tensor_tensor(h[:, it], half(UG_BANK[it % 2], 0), wsu[:, it:it + 1], sg[:, it % 2],
                                               ALU.mult, ALU.mult).then_inc(h_ready, 1)

            def residual2(g):
                dve.wait_ge(dn_psum, g + 1)
                wait_last(dve, out_ready, g)
                dve.wait_ge(y_ready, g + 1)
                nc.vector.tensor_tensor(res2[:], halves(FFN_BANK), y[:], ALU.add).then_inc(res2_ready, 1)
                dve.wait_ge(res2_ready, g + 1)
                for j in range(J):
                    last = nc.vector.bn_stats(stat2[:, j], res2[:, j])
                last.then_inc(stat2_done, 1)
                dve.wait_ge(stat2_done, g + 1)
                moments(g, stat2, m2, C, LN_EPS, mv2_done, var2_ready)

            def norm2(g):
                dve.wait_ge(rs2_ready, g + 1)
                wait_last(dve, stored, 16 * g)
                for j in range(J):
                    last = nc.vector.tensor_scalar(outs[:, j], res2[:, j], m2["mean"][:, j:j + 1], rs2[:, j:j + 1],
                                                   ALU.subtract, ALU.mult)
                last.then_inc(out_ready, 1)

            def group(g, f=None):
                token_mix(g)
                mix(g, 0)
                if f is not None:
                    y_butterfly(f)
                for i in range(1, 5):
                    mix(g, i)
                if f is None:
                    rotate_down()
                    scale_down()
                for n in range(7):
                    if f is not None:
                        swiglu(f, n)
                    level(g, n)
                if f is not None:
                    swiglu(f, 7)
                for j in range(J):
                    state(g, j)
                group_norm(g)
                if f is not None:
                    residual2(f)
                    norm2(f)
                residual1(g)
                norm1(g)

            dve.wait_ge(L["vec"], 16)
            nc.vector.tensor_scalar(wsu[:], vec[:, VEC["ws_up"]:VEC["ws_up"] + 2 * IT], FFN_SCALE, None, ALU.mult)
            nc.vector.tensor_scalar(sdu[:], vec[:, VEC["su_dp"]:VEC["su_dp"] + IT],
                                    1.0 / INTER ** 0.5, None, ALU.mult).then_inc(scales_ready, 1)
            dve.wait_ge(scales_ready, 1)
            dve.wait_ge(L["masks"], 16)
            dve.wait_ge(zeroed, 1)
            group(0)
            group(1, 0)
            with dve.Fori(2, G) as g:
                group(g, g - 1)
            y_butterfly(G - 1)
            for it in range(IT):
                swiglu(G - 1, it)
            residual2(G - 1)
            norm2(G - 1)

        @block.tensor
        def _(pe):
            def z(g):
                pe.wait_ge(xxx_ready, g + 1)
                wait_last(pe, S_ready, 2 * g)
                for c in range(CH):
                    nc.tensor.matmul(bank[0][:, 0:TG], w1[:, c, 0:P], xxx[:, c], start=c == 0, stop=c == CH - 1)
                for c in range(CH):
                    last = nc.tensor.matmul(bank[0][0:DMIX, TG:2 * TG], w1[:, c, P:P + DMIX], xxx[:, c], start=c == 0,
                                            stop=c == CH - 1)
                last.then_inc(z_psum, 1)

            def mix(g, i):
                n = MIXES[i]
                f = PART[n]
                if i == 0:
                    pe.wait_ge(z_tanh, g + 1)
                wait_last(pe, {"w": nT_ready, "k": norm_ready, "r": res_ready, "v": norm_ready, "g": z_tanh}[n],
                           g + 1 if n == "g" else g)
                lo, hi = (0, DMIX) if n == "g" else (f * DMIX, (f + 1) * DMIX)
                for c in range(CH):
                    w, zz = (w2g, ztg) if n == "g" else (w2, zt)
                    last = nc.tensor.matmul(half(MIX_BANK[n], c), w[lo:hi, c * P:(c + 1) * P], zz[lo:hi, :], start=True,
                                            stop=True, tile_position=(lo, 0))
                last.then_inc(mix_psum, 1)

            def dec1(g):
                pe.wait_ge(xm_ready, 5 * g + 1)
                for c in range(CH):
                    last = nc.tensor.matmul(bank[1][0:DDEC, 0:TG], dw1[:, c], xm["w"][:, c], start=c == 0,
                                            stop=c == CH - 1)
                last.then_inc(dec1_psum, 1)

            def dec2(g):
                pe.wait_ge(dec1_tanh, g + 1)
                pe.wait_ge(mixed_ready, 5 * g + 3)
                for c in range(CH):
                    last = nc.tensor.matmul(half(3, c), dw2[:, c * P:(c + 1) * P], tdec[:], start=True, stop=True)
                last.then_inc(dec2_psum, 1)

            def channels(g, n, i, b, done):
                pe.wait_ge(xm_ready, 5 * g + i + 1)
                if n == "r":
                    pe.wait_ge(mixed_ready, 5 * g + 4)
                for a in range(CH):
                    for c in range(CH):
                        last = nc.tensor.matmul(half(b, a), proj[n][:, c, a * P:(a + 1) * P], xm[n][:, c],
                                                start=c == 0, stop=c == CH - 1)
                last.then_inc(done, 1)

            def v(g):
                pe.wait_ge(xm_ready, 5 * g + 4)
                pe.wait_ge(mixed_ready, 5 * g + 5)
                for j in range(J):
                    for c in range(CH):
                        last = nc.tensor.matmul(half(0, j), xm["v"][:, c, j * Q:(j + 1) * Q], proj["v"][:, c],
                                                start=c == 0, stop=c == CH - 1)
                last.then_inc(v_psum, 1)

            def head(src, c, e, j):
                return src[e * HS:(e + 1) * HS, c, j * Q:(j + 1) * Q]

            def level(g, n):
                Ln = LEVELS[n]
                if n == 0:
                    pe.wait_ge(k_ready, g + 1)
                    pe.wait_ge(r_ready, g + 1)
                    pe.wait_ge(w_ready, g + 1)
                    pe.wait_ge(v_ready, g + 1)
                    for j in range(J):
                        for c in range(CH):
                            for e in range(2):
                                a = j * CH + c
                                nc.tensor.matmul(bank[DIAG_BANKS[e]][:, a * Q:(a + 1) * Q], head(uk, c, e, j),
                                                 head(rq, c, e, j), start=True, stop=True)
                else:
                    pe.wait_ge(q_scaled, 7 * g + n)
                    pe.wait_ge(k_scaled, 7 * g + n)
                    if n == 1:
                        pe.wait_ge(diag_copied, g + 1)
                    else:
                        pe.wait_ge(A_copied, 7 * g + n - 1)
                for j in range(J):
                    for c in range(CH):
                        for e in range(2):
                            a = j * CH + c
                            qq = head(rq, c, e, j).rearrange("p (b e l) -> p b e l", e=2, l=Ln)[:, :, 1]
                            last = nc.tensor.matmul(
                                bank[LEVEL_BANKS[n % 2][e]][:, a * HALF:(a + 1) * HALF].rearrange(
                                    "p (b l) -> p b l", l=Ln), head(kq, c, e, j), qq, start=True, stop=True)
                last.then_inc(level_psum, 1)

            def k_transpose(g):
                pe.wait_ge(k_scaled, 7 * g + 7)
                pe.wait_ge(g_ready, g + 1)
                for j in range(J):
                    for c in range(CH):
                        a = j * CH + c
                        last = nc.tensor.transpose(bank[1][:, a * P:(a + 1) * P], kq[:, c, j * Q:(j + 1) * Q], ident[:])
                last.then_inc(kT_psum, 1)

            def chunk(g, j):
                if j == 0:
                    pe.wait_ge(A_copied, 7 * g + 7)
                    pe.wait_ge(q_scaled, 7 * g + 7)
                wait_last(pe, S_ready, 2 * g + j)
                b = OUT_BANK[j]
                for c in range(CH):
                    nc.tensor.matmul(bank[b][:, c * P:(c + 1) * P], rq[:, c, j * Q:(j + 1) * Q], S[:, c], start=True,
                                     stop=False)
                    for e in range(2):
                        hh = 2 * c + e
                        last = nc.tensor.matmul(bank[b][:, hh * HS:(hh + 1) * HS], A[e][:, j, c],
                                                vs[:, j, hh * HS:(hh + 1) * HS], start=False, stop=e == 1)
                last.then_inc(o_psum, 1)
                if j == 0:
                    pe.wait_ge(kT_ready, g + 1)
                for c in range(CH):
                    last = nc.tensor.matmul(bank[STATE_BANK[j]][:, c * P:(c + 1) * P], kT[:, j, c],
                                            vs[:, j, c * P:(c + 1) * P], start=True, stop=True)
                last.then_inc(st_psum, 1)

            def norm_transpose(g):
                pe.wait_ge(norm_ready, g + 1)
                pe.wait_ge(kT_ready, g + 1)
                for c in range(CH):
                    for j in range(J):
                        last = nc.tensor.transpose(bank[1][:, c * TG + j * Q:c * TG + (j + 1) * Q],
                                                   norm[:, j, c * P:(c + 1) * P], ident[:])
                last.then_inc(nT_psum, 1)

            def w_o(g):
                pe.wait_ge(og_ready, g + 1)
                pe.wait_ge(S_ready, 2 * g + 1)
                for j in range(J):
                    for c in range(CH):
                        last = nc.tensor.matmul(half(3, j), og[:, c, j * Q:(j + 1) * Q], proj["o"][:, c], start=c == 0,
                                                stop=c == CH - 1)
                last.then_inc(wo_psum, 1)

            def rotate_down():
                pe.wait_ge(L["const"], 32)
                pe.wait_ge(wd_step, 3)
                for i in range(IT // 2):
                    if i >= 2:
                        pe.wait_ge(wd_ready, i - 1)
                    nc.tensor.matmul(bank[UG_BANK[i % 2]][:], had[:],
                                     wd_tmp[:, 2 * i:2 * i + 2].rearrange("p a c -> p (a c)"), start=True,
                                     stop=True).then_inc(wd_psum, 1)

            def y_transpose(g):
                pe.wait_ge(y_ready, g + 1)
                wait_last(pe, res2_ready, g)
                for c in range(CH):
                    for j in range(J):
                        last = nc.tensor.transpose(bank[FFN_BANK][:, c * TG + j * Q:c * TG + (j + 1) * Q],
                                                   y[:, j, c * P:(c + 1) * P], ident[:])
                last.then_inc(yT_psum, 1)

            def rotate_x(g):
                pe.wait_ge(yu_ready, g + 1)
                nc.tensor.matmul(bank[FFN_BANK][:], had[:], yu[:].rearrange("p c t -> p (c t)"), start=True,
                                 stop=True).then_inc(xh_psum, 1)

            def up_gate(g, it):
                if it == 0:
                    pe.wait_ge(xh_ready, g + 1)
                wait_last(pe, h_ready, 8 * g + max(it - 1, 0))
                b = UG_BANK[it % 2]
                for e, w in enumerate((wup, wgate)):
                    for c in range(CH):
                        last = nc.tensor.matmul(half(b, e), w[:, c, it * P:(it + 1) * P], xh[:, c], start=c == 0,
                                                stop=c == CH - 1)
                last.then_inc(ug_psum, 1)

            def down(g, j):
                if j == 0:
                    pe.wait_ge(h_ready, 8 * g + 8)
                for it in range(IT):
                    last = nc.tensor.matmul(half(FFN_BANK, j), h[:, it, j * Q:(j + 1) * Q], wdown[:, it],
                                            start=it == 0, stop=it == IT - 1)
                if j == J - 1:
                    last.then_inc(dn_psum, 1)

            def loaded(name, count=16, first=True):
                if first:
                    pe.wait_ge(L[name], count)

            def group(g, f=None):
                first = f is None
                z(g)
                if f is not None:
                    y_transpose(f)
                loaded("w2", 32, first)
                mix(g, 0)
                if f is not None:
                    rotate_x(f)
                for i in range(1, 5):
                    mix(g, i)
                loaded("dw", 32, first)
                dec1(g)
                loaded("W_k", 16, first)
                channels(g, "k", 1, 2, k_psum)
                dec2(g)
                loaded("W_r", 16, first)
                channels(g, "r", 2, 4, r_psum)
                loaded("W_v", 16, first)
                v(g)
                loaded("W_g", 16, first)
                channels(g, "g", 4, 1, g_psum)
                if f is None:
                    rotate_down()
                for n in range(7):
                    if f is not None:
                        up_gate(f, n)
                    level(g, n)
                if f is not None:
                    up_gate(f, 7)
                loaded("const", 32, first)
                k_transpose(g)
                chunk(g, 0)
                if f is not None:
                    down(f, 0)
                chunk(g, 1)
                if f is not None:
                    down(f, 1)
                norm_transpose(g)
                loaded("W_o", 16, first)
                w_o(g)

            pe.wait_ge(L["w1"], 16)
            group(0)
            pe.wait_ge(L["wug"], 32)
            pe.wait_ge(wd_ready, IT // 2)
            group(1, 0)
            with pe.Fori(2, G) as g:
                group(g, g - 1)
            y_transpose(G - 1)
            rotate_x(G - 1)
            for it in range(IT):
                up_gate(G - 1, it)
            for j in range(J):
                down(G - 1, j)


def _masks(np):
    s = np.arange(Q)[:, None]
    parts = [s == np.arange(Q)[None, :]]
    for n in LEVELS:
        t = np.arange(Q)
        t = t[(t // n) % 2 == 1][None, :]
        parts.append((s // (2 * n) == t // (2 * n)) & ((s // n) % 2 == 0))
    return np.concatenate(parts, axis=1).astype(np.float32)


def _hadamard(np):
    m = np.ones((1, 1), np.float32)
    while m.shape[0] < P:
        m = np.block([[m, m], [m, -m]])
    return m


def kernel(**inputs):
    import numpy as np
    import concourse.bacc as _bacc
    from concourse import mybir as _mybir
    from concourse.bass_utils import run_bass_kernel_spmd as _run

    a = {k: np.asarray(v) for k, v in inputs.items()}
    A_, F_ = "L0_attn_", "L0_ffn_"

    def rows(m):
        return m.reshape(-1, P, m.shape[1]).transpose(1, 0, 2)

    def cols(v):
        return v.reshape(-1, P).T

    x = a[A_ + "hidden"][0]
    w2 = a[A_ + "time_maa_w2"]
    vec = [cols(a[A_ + "time_maa_" + n]) for n in "xwkrvg"]
    vec += [cols(a[A_ + n]) for n in ("time_decay", "time_faaaa", "ln_gamma", "ln_beta")]
    vec += [cols(a[F_ + n]) for n in ("SU_ug", "Wscale_ug", "SU_dp")]
    arrays = {
        "xT": rows(x.T), "xtok": rows(x), "vec": np.concatenate(vec, axis=1),
        "w1": rows(a[A_ + "time_maa_w1"]), "w2": w2[0:4].reshape(P, C), "w2g": w2[4],
        "dw1": rows(a[A_ + "time_decay_w1"]), "dw2": a[A_ + "time_decay_w2"],
        "wup": rows(a[F_ + "W_up"].T), "wgate": rows(a[F_ + "W_gate"].T), "wdown": rows(a[F_ + "W_down"].T),
        "wsrow": a[F_ + "Wscale_dp"].reshape(1, C),
        "had": _hadamard(np), "ident": np.eye(P, dtype=np.float32), "masks": _masks(np),
    }
    for n in "krvgo":
        arrays["W_" + n] = rows(a[A_ + "W_" + n].T)
    arrays = {k: np.ascontiguousarray(v) for k, v in arrays.items()}

    nc = _bacc.Bacc("TRN2", target_bir_lowering=False, num_devices=1)
    d = {k: nc.dram_tensor(f"{k}_dram", v.shape, _mybir.dt.from_np(v.dtype), kind="ExternalInput").ap()
         for k, v in arrays.items()}
    out = nc.dram_tensor("out_dram", (1, T, C), F32, kind="ExternalOutput").ap()
    d["out"] = out.rearrange("o (j p) c -> p (o j) c", p=P)
    build(nc, d)
    r = _run(nc, [{f"{k}_dram": v for k, v in arrays.items()}], core_ids=[0])
    return r.results[0]["out_dram"]
```

```python
from contextlib import ExitStack

import concourse.bass as bass
from concourse import mybir

F32 = mybir.dt.float32
F32R = mybir.dt.float32r
U32 = mybir.dt.uint32
ACT = mybir.ActivationFunctionType
ALU = mybir.AluOpType

T = 1024
C = 256
P = 128
CH = C // P
HS = 64
HEADS = C // HS
TG = 256
G = T // TG
Q = 128
J = TG // Q
DMIX = 32
DDEC = 64
INTER = 1024
IT = INTER // P
LEVELS = [1, 2, 4, 8, 16, 32, 64]
HALF = Q // 2
FFN_SCALE = 64.0
GN_EPS = 1e-05 * 8.0 ** 2
LN_EPS = 1e-05

VEC = {}
_at = 0
for _name, _n in [("maa_x", CH), ("maa_w", CH), ("maa_k", CH), ("maa_r", CH), ("maa_v", CH), ("maa_g", CH),
                  ("decay", CH), ("u", CH), ("gamma", CH), ("beta", CH), ("su_ug", CH), ("ws_up", IT),
                  ("ws_gate", IT), ("su_dp", IT)]:
    VEC[_name] = _at
    _at += _n
VCOLS = _at

PART = {"w": 0, "k": 1, "v": 2, "r": 3, "g": 4}
MIXES = ["w", "k", "r", "v", "g"]
Z_BANK = 5
MIX_BANK = {"w": 6, "k": 1, "r": 0, "v": 7, "g": 5}
DEC1_BANK = 6
DEC2_BANK = 0
PROJ_BANK = {"k": 1, "r": 4, "v": 5, "g": 6}
LEVEL_BANK = [3, 4]
DIAG_BANK = 0
KT_BANK = 1
OUT_BANK = 2
STATE_BANK = [0, 4]
NT_BANK = 3
WO_BANK = 2
UG_BANK = [5, 6]
WD_BANK = 2
FFN_BANK = 7


def wait_last(eng, sem, value):
    if not isinstance(value, int) or value > 0:
        eng.wait_ge(sem, value)


def build(nc, d):
    with ExitStack() as ctx:
        def sb(name, shape, dt=F32):
            return ctx.enter_context(nc.sbuf_tensor(name, shape, dt))

        def sem(name):
            return ctx.enter_context(nc.semaphore(name))

        def moment_tiles(name, n):
            return {k: sb(f"{name}_{k}", [P, n]) for k in ("sum", "diff", "m2", "sq", "mean", "var", "m2n")}

        bank = [ctx.enter_context(nc.psum_tensor(f"bank{i}", [P, 512], F32)) for i in range(8)]

        xT = sb("xT", [P, CH, TG + 1])
        xtok = sb("xtok", [P, J, C])
        vec = sb("vec", [P, VCOLS])
        w1 = sb("w1", [P, CH, 5 * DMIX])
        w2 = sb("w2", [P, C])
        w2g = sb("w2g", [DMIX, C])
        dw1 = sb("dw1", [P, CH, DDEC])
        dw2 = sb("dw2", [DDEC, C])
        proj = {n: sb(f"W_{n}", [P, CH, C]) for n in "krvgo"}
        wup = sb("wup", [P, CH, INTER])
        wgate = sb("wgate", [P, CH, INTER])
        wdown = sb("wdown", [P, IT, C])
        wd_tmp = sb("wd_tmp", [P, IT, C])
        wsrow = sb("wsrow", [P, C])
        had = sb("had", [P, P])
        ident = sb("ident", [P, P])
        heads = sb("heads", [P, 2])
        masks = sb("masks", [P, HALF * len(LEVELS)])
        neghalf = sb("neghalf", [P, J * HEADS])

        xx = sb("xx", [P, CH, TG])
        xxx = sb("xxx", [P, CH, TG])
        mixed = sb("mixed", [P, 2, CH, TG])
        xm = {n: sb(f"x_{n}", [P, CH, TG]) for n in MIXES}
        zt = sb("zt", [P, TG])
        ztg = sb("ztg", [DMIX, TG])
        tdec = sb("tdec", [DDEC, TG])
        edec = sb("edec", [P, CH, TG])
        wdec = [sb(f"wdec{L}", [P, CH, TG // L]) for L in LEVELS + [Q]]
        kq = sb("kq", [P, CH, TG])
        rq = sb("rq", [P, CH, 2, TG])
        ruk = sb("ruk", [P, CH, TG])
        bonus = sb("bonus", [P, J * CH, 2])
        vs = sb("vs", [P, J, C])
        gT = sb("gT", [P, CH, TG])
        A = sb("A", [P, J * CH, 2, Q])
        kT = sb("kT", [P, J, CH, P])
        S = sb("S", [P, CH, P])
        gstat = sb("gstat", [P, J * HEADS, 6])
        gm = moment_tiles("gm", J * HEADS)
        grs = sb("grs", [P, J * HEADS])
        norm = sb("norm", [P, J, C])
        nT = sb("nT", [P, CH, TG])
        og = sb("og", [P, CH, TG])
        res = sb("res", [P, J, C])
        stat1 = sb("stat1", [P, J, 6])
        m1 = moment_tiles("m1", J)
        rs1 = sb("rs1", [P, J])
        y = sb("y", [P, J, C])

        wsu = sb("wsu", [P, 2 * IT])
        sdu = sb("sdu", [P, IT])
        ya = sb("ya", [P, TG])
        yu = sb("yu", [P, CH, TG])
        xh = [sb(f"xh_{n}", [P, CH, TG], F32R) for n in ("hi", "lo")]
        wu = [sb(f"wu_{n}", [P, CH, INTER], F32R) for n in ("hi", "lo")]
        wg = [sb(f"wg_{n}", [P, CH, INTER], F32R) for n in ("hi", "lo")]
        sg = sb("sg", [P, 2, TG])
        h = sb("h", [P, IT, TG])
        res2 = sb("res2", [P, J, C])
        stat2 = sb("stat2", [P, J, 6])
        m2 = moment_tiles("m2", J)
        rs2 = sb("rs2", [P, J])
        outs = sb("outs", [P, J, C])

        L = {n: sem(f"load_{n}") for n in ( "vec", "w1", "w2", "dw", "W_k", "W_r", "W_v", "W_g",
                                           "W_o", "wug", "wdown", "wsrow", "const", "heads", "masks")}
        zeroed = sem("zeroed")
        xT_loaded = sem("xT_loaded")
        xtok_loaded = sem("xtok_loaded")
        xxx_ready = sem("xxx_ready")
        z_psum = sem("z_psum")
        z_tanh = sem("z_tanh")
        mix_psum = sem("mix_psum")
        mixed_ready = sem("mixed_ready")
        xm_ready = sem("xm_ready")
        dec1_psum = sem("dec1_psum")
        dec1_tanh = sem("dec1_tanh")
        dec2_psum = sem("dec2_psum")
        exp_ready = sem("exp_ready")
        w_ready = sem("w_ready")
        k_psum = sem("k_psum")
        r_psum = sem("r_psum")
        v_psum = sem("v_psum")
        g_psum = sem("g_psum")
        k_ready = sem("k_ready")
        r_ready = sem("r_ready")
        v_ready = sem("v_ready")
        g_ready = sem("g_ready")
        level_psum = sem("level_psum")
        q_scaled = sem("q_scaled")
        k_scaled = sem("k_scaled")
        wprod = sem("wprod")
        ruk_ready = sem("ruk_ready")
        bonus_psum = sem("bonus_psum")
        bonus_copied = sem("bonus_copied")
        diag_written = sem("diag_written")
        A_copied = sem("A_copied")
        kT_psum = sem("kT_psum")
        kT_ready = sem("kT_ready")
        o_psum = sem("o_psum")
        st_psum = sem("st_psum")
        S_ready = sem("S_ready")
        gvar_ready = sem("gvar_ready")
        grs_ready = sem("grs_ready")
        norm_ready = sem("norm_ready")
        nT_psum = sem("nT_psum")
        nT_ready = sem("nT_ready")
        og_ready = sem("og_ready")
        wo_psum = sem("wo_psum")
        res_ready = sem("res_ready")
        var1_ready = sem("var1_ready")
        rs1_ready = sem("rs1_ready")
        y_ready = sem("y_ready")
        scales_ready = sem("scales_ready")
        wd_step = sem("wd_step")
        wd_psum = sem("wd_psum")
        wd_ready = sem("wd_ready")
        yT_psum = sem("yT_psum")
        ya_ready = sem("ya_ready")
        yu_ready = sem("yu_ready")
        xh_psum = sem("xh_psum")
        xh_ready = sem("xh_ready")
        xl_ready = sem("xl_ready")
        whi_ready = sem("whi_ready")
        wu_lo_ready = sem("wu_lo_ready")
        wg_lo_ready = sem("wg_lo_ready")
        ug_psum = sem("ug_psum")
        silu_ready = sem("silu_ready")
        h_ready = sem("h_ready")
        dn_psum = sem("dn_psum")
        res2_ready = sem("res2_ready")
        var2_ready = sem("var2_ready")
        rs2_ready = sem("rs2_ready")
        out_ready = sem("out_ready")
        stored = sem("stored")
        xx_done = sem("xx_done")
        gstat_done = sem("gstat_done")
        gmv_done = sem("gmv_done")
        stat1_done = sem("stat1_done")
        mv1_done = sem("mv1_done")
        stat2_done = sem("stat2_done")
        mv2_done = sem("mv2_done")

        def vcol(name, i, lo=0, hi=P):
            return vec[lo:hi, VEC[name] + i:VEC[name] + i + 1]

        now, before = xT[:, :, 1:TG + 1], xT[:, :, 0:TG]

        def flat(t):
            return t[:].rearrange("p c t -> p (c t)")

        def half(b, c):
            return bank[b][:, c * TG:(c + 1) * TG]

        def halves(b):
            return bank[b][:, :].rearrange("p (c t) -> p c t", c=2)

        block = ctx.enter_context(nc.Block())

        @block.sync
        def _(sp):
            sp.dma_start(now, d["xT"][:, :, 0:TG]).then_inc(xT_loaded, 16)
            sp.dma_start(w1[:], d["w1"]).then_inc(L["w1"], 16)
            sp.dma_start(dw1[:], d["dw1"]).then_inc(L["dw"], 16)
            sp.dma_start(proj["k"][:], d["W_k"]).then_inc(L["W_k"], 16)
            sp.dma_start(proj["r"][:], d["W_r"]).then_inc(L["W_r"], 16)
            sp.dma_start(masks[:], d["masks"]).then_inc(L["masks"], 16)
            sp.dma_start(xtok[:], d["xtok"][:, 0:J, :]).then_inc(xtok_loaded, 16)
            sp.dma_start(wup[:], d["wup"]).then_inc(L["wug"], 16)

            def load_xT(g):
                wait_last(sp, xm_ready, 5 * g)
                sp.dma_start(xT[:], d["xT"][:, :, bass.ds(g * TG - 1, TG + 1)]).then_inc(xT_loaded, 16)

            def load_xtok(g):
                wait_last(sp, res_ready, g)
                sp.dma_start(xtok[:], d["xtok"][:, bass.ds(g * J, J), :]).then_inc(xtok_loaded, 16)

            def store(g):
                sp.wait_ge(out_ready, g + 2)
                sp.dma_start(d["out"][:, bass.ds(g * J, J), :], outs[:]).then_inc(stored, 16)

            load_xT(1)
            load_xtok(1)
            load_xT(2)
            with sp.Fori(1, G - 2) as g:
                load_xT(g + 2)
                store(g - 1)
                load_xtok(g + 1)
            store(G - 3)
            load_xtok(G - 1)
            store(G - 2)
            store(G - 1)
            sp.wait_ge(stored, 16 * (G + 1))

        @block.gpsimd
        def _(pool):
            nc.gpsimd.memset(xT[:, :, 0:1], 0.0)
            nc.gpsimd.memset(neghalf[:], -0.5)
            nc.gpsimd.memset(S[:], 0.0)
            nc.gpsimd.memset(rq[:], 0.0).then_inc(zeroed, 1)
            pool.wait_ge(zeroed, 1)
            for s, n in [(yT_psum, 1), (ya_ready, 1), (yu_ready, 1), (xh_psum, 1), (xh_ready, 1), (xl_ready, 1), (ug_psum, IT),
                         (silu_ready, IT), (h_ready, IT), (dn_psum, 1), (res2_ready, 1), (var2_ready, 1),
                         (rs2_ready, 1), (out_ready, 1), (stored, 16)]:
                pool.sem_inc(s, n)

            def mix_add(g, i):
                pool.wait_ge(mixed_ready, 5 * g + i + 1)
                wait_last(pool, {"w": dec1_psum, "k": k_psum, "r": r_psum, "v": v_psum, "g": g_psum}[MIXES[i]], g)
                nc.gpsimd.tensor_tensor(xm[MIXES[i]][:], mixed[:, i % 2], now, ALU.add).then_inc(xm_ready, 1)

            def scale_k(g, n):
                Ln = LEVELS[n]
                pool.wait_ge(level_psum, 7 * g + n + 1)
                if n == 0:
                    pool.wait_ge(w_ready, g + 1)
                else:
                    pool.wait_ge(wprod, 7 * g + n)
                    pool.wait_ge(k_scaled, 7 * g + n)
                kk = kq[:].rearrange("p c (b e l) -> p (c b) e l", e=2, l=Ln)[:, :, 0]
                ww = wdec[n][:].rearrange("p c (b e) -> p (c b) e", e=2)[:, :, 1:2].to_broadcast([P, CH * TG // (2 * Ln), Ln])
                nc.gpsimd.tensor_tensor(kk, kk, ww, ALU.mult).then_inc(k_scaled, 1)

            def group_rsqrt(g):
                pool.wait_ge(gvar_ready, g + 1)
                wait_last(pool, norm_ready, g)
                nc.gpsimd.tensor_tensor(grs[:], gm["var"][:], neghalf[:], ALU.pow).then_inc(grs_ready, 1)

            def gate(g):
                pool.wait_ge(nT_ready, g + 1)
                pool.wait_ge(g_ready, g + 1)
                wait_last(pool, wo_psum, g)
                nc.gpsimd.tensor_tensor(og[:], nT[:], gT[:], ALU.mult).then_inc(og_ready, 1)

            def rsqrt1(g):
                pool.wait_ge(var1_ready, g + 1)
                wait_last(pool, y_ready, g)
                nc.gpsimd.tensor_tensor(rs1[:], m1["var"][:], neghalf[:, 0:J], ALU.pow).then_inc(rs1_ready, 1)

            def rsqrt2(r):
                pool.wait_ge(var2_ready, r + 1)
                pool.wait_ge(out_ready, r)
                nc.gpsimd.tensor_tensor(rs2[:], m2["var"][:], neghalf[:, 0:J], ALU.pow).then_inc(rs2_ready, 1)

            def turn(g, first=False, last=False):
                for n in range(7):
                    scale_k(g, n)
                    if first and 1 <= n <= 5:
                        mix_add(1, n - 1)
                if first:
                    pool.wait_ge(whi_ready, 2)
                    nc.gpsimd.tensor_tensor(wg[1][:], wgate[:], wg[0][:].bitcast(F32), ALU.subtract).then_inc(
                        wg_lo_ready, 1)
                if not first and not last:
                    rsqrt2(g)
                group_rsqrt(g)
                if not first and not last:
                    for i in range(4):
                        mix_add(g + 1, i)
                gate(g)
                if last:
                    rsqrt2(g)
                elif not first:
                    mix_add(g + 1, 4)
                rsqrt1(g)

            for i in range(5):
                mix_add(0, i)
            turn(0, first=True)
            with pool.Fori(1, G - 1) as g:
                turn(g)
            turn(G - 1, last=True)
            rsqrt2(G)

        @block.scalar
        def _(act):
            act.dma_start(vec[:], d["vec"]).then_inc(L["vec"], 16)
            act.dma_start(w2[:], d["w2"]).then_inc(L["w2"], 16)
            act.dma_start(w2g[:], d["w2g"]).then_inc(L["w2"], 16)
            act.dma_start(dw2[:], d["dw2"]).then_inc(L["dw"], 16)
            act.dma_start(proj["v"][:], d["W_v"]).then_inc(L["W_v"], 16)
            act.dma_start(proj["g"][:], d["W_g"]).then_inc(L["W_g"], 16)
            act.dma_start(had[:], d["had"]).then_inc(L["const"], 16)
            act.dma_start(ident[:], d["ident"]).then_inc(L["const"], 16)
            act.dma_start(heads[:], d["heads"]).then_inc(L["heads"], 16)
            act.dma_start(wdown[:], d["wdown"]).then_inc(L["wdown"], 16)
            act.dma_start(wsrow[:], d["wsrow"].to_broadcast([P, C])).then_inc(L["wsrow"], 16)
            act.dma_start(proj["o"][:], d["W_o"]).then_inc(L["W_o"], 16)
            act.dma_start(wgate[:], d["wgate"]).then_inc(L["wug"], 16)

            def z(g):
                act.wait_ge(z_psum, g + 1)
                wait_last(act, mix_psum, 5 * g)
                nc.scalar.activation(zt[:], half(Z_BANK, 0), ACT.Tanh)
                nc.scalar.activation(ztg[:], bank[Z_BANK][0:DMIX, TG:2 * TG], ACT.Tanh).then_inc(z_tanh, 1)

            def decay_tanh(g):
                act.wait_ge(dec1_psum, g + 1)
                wait_last(act, dec2_psum, g)
                nc.scalar.activation(tdec[:], bank[DEC1_BANK][0:DDEC, 0:TG], ACT.Tanh).then_inc(dec1_tanh, 1)

            def k_out(g):
                act.wait_ge(k_psum, g + 1)
                wait_last(act, kT_psum, g)
                wait_last(act, k_scaled, 7 * g)
                nc.scalar.copy(kq[:], halves(PROJ_BANK["k"])).then_inc(k_ready, 1)

            def decay(g):
                act.wait_ge(dec2_psum, g + 1)
                wait_last(act, w_ready, g)
                for c in range(CH):
                    last = nc.scalar.activation(edec[:, c], half(DEC2_BANK, c), ACT.Exp, bias=vcol("decay", c))
                last.then_inc(exp_ready, 1)
                act.wait_ge(exp_ready, g + 1)
                wait_last(act, wprod, 7 * g)
                wait_last(act, k_scaled, 7 * g)
                nc.scalar.activation(wdec[0][:], edec[:], ACT.Exp, scale=-1.0).then_inc(w_ready, 1)

            def r_out(g):
                act.wait_ge(r_psum, g + 1)
                wait_last(act, q_scaled, 7 * g)
                wait_last(act, o_psum, 2 * g)
                for e in range(2):
                    lo, hi = e * HS, (e + 1) * HS
                    last = nc.scalar.copy(rq[lo:hi, :, e], halves(PROJ_BANK["r"])[lo:hi])
                last.then_inc(r_ready, 1)

            def v_out(g):
                act.wait_ge(v_psum, g + 1)
                wait_last(act, st_psum, 2 * g)
                nc.scalar.copy(vs[:], halves(PROJ_BANK["v"])).then_inc(v_ready, 1)

            def g_out(g):
                act.wait_ge(g_psum, g + 1)
                wait_last(act, og_ready, g)
                nc.scalar.activation(gT[:], halves(PROJ_BANK["g"]), ACT.Silu).then_inc(g_ready, 1)

            def bonus_out(g):
                act.wait_ge(bonus_psum, g + 1)
                wait_last(act, diag_written, g)
                nc.scalar.copy(bonus[:], bank[DIAG_BANK][:, 0:J * CH * 2].rearrange("p (a e) -> p a e", e=2)).then_inc(
                    bonus_copied, 1)

            def kT_out(g):
                act.wait_ge(kT_psum, g + 1)
                wait_last(act, st_psum, 2 * g)
                nc.scalar.copy(kT[:], bank[KT_BANK][:].rearrange("p (j c n) -> p j c n", j=J, c=CH)).then_inc(kT_ready, 1)

            def affine(g):
                act.wait_ge(nT_psum, g + 1)
                wait_last(act, og_ready, g)
                for c in range(CH):
                    last = nc.scalar.activation(nT[:, c], half(NT_BANK, c), ACT.Identity, bias=vcol("beta", c),
                                                scale=vcol("gamma", c))
                last.then_inc(nT_ready, 1)

            def y_signed(r):
                act.wait_ge(yT_psum, r + 1)
                act.wait_ge(yu_ready, r)
                nc.scalar.activation(ya[:], half(FFN_BANK, 0), ACT.Copy, scale=vcol("su_ug", 0)).then_inc(ya_ready, 1)

            def x_rotated(r):
                act.wait_ge(xh_psum, r + 1)
                act.wait_ge(ug_psum, IT * r)
                s = 1.0 / (C ** 0.5 * FFN_SCALE)
                nc.scalar.mul(xh[0][:, 0], half(FFN_BANK, 0), s)
                nc.scalar.mul(xh[0][:, 1], half(FFN_BANK, 1), -s).then_inc(xh_ready, 1)

            def silu(r, it):
                act.wait_ge(ug_psum, IT * r + it + 1)
                act.wait_ge(h_ready, IT * r + max(it - 1, 0))
                nc.scalar.activation(sg[:, it % 2], half(UG_BANK[it % 2], 1), ACT.Silu,
                                     scale=wsu[:, IT + it:IT + it + 1]).then_inc(silu_ready, 1)

            def split_high():
                act.wait_ge(L["wug"], 32)
                nc.scalar.copy(wu[0][:], wup[:]).then_inc(whi_ready, 1)
                nc.scalar.copy(wg[0][:], wgate[:]).then_inc(whi_ready, 1)

            def head(g):
                k_out(g)
                decay(g)
                r_out(g)
                v_out(g)
                g_out(g)

            def turn(g, first=False, last=False):
                bonus_out(g)
                if first:
                    z(1)
                    split_high()
                    decay_tanh(1)
                else:
                    x_rotated(g)
                    for it in range(IT):
                        silu(g, it)
                kT_out(g)
                if not first and not last:
                    z(g + 1)
                affine(g)
                if not last:
                    if not first:
                        decay_tanh(g + 1)
                    head(g + 1)
                y_signed(g + 1)

            act.wait_ge(L["vec"], 16)
            act.wait_ge(zeroed, 1)
            z(0)
            decay_tanh(0)
            head(0)
            turn(0, first=True)
            act.wait_ge(scales_ready, 1)
            with act.Fori(1, G - 1) as g:
                turn(g)
            turn(G - 1, last=True)
            x_rotated(G)
            for it in range(IT):
                silu(G, it)

        @block.vector
        def _(dve):
            def token_mix(g):
                dve.wait_ge(xT_loaded, 16 * g + 16)
                nc.vector.tensor_tensor(xx[:], before, now, ALU.subtract).then_inc(xx_done, 1)
                dve.wait_ge(xx_done, g + 1)
                wait_last(dve, z_psum, g)
                for c in range(CH):
                    last = nc.vector.scalar_tensor_tensor(xxx[:, c], xx[:, c], vcol("maa_x", c), now[:, c],
                                                          ALU.mult, ALU.add)
                last.then_inc(xxx_ready, 1)

            def mix(g, i):
                dve.wait_ge(mix_psum, 5 * g + i + 1)
                wait_last(dve, xm_ready, 5 * g + max(i - 1, 0))
                for c in range(CH):
                    last = nc.vector.scalar_tensor_tensor(mixed[:, i % 2, c], half(MIX_BANK[MIXES[i]], c),
                                                          vcol("maa_" + MIXES[i], c), xx[:, c], ALU.add, ALU.mult)
                last.then_inc(mixed_ready, 1)

            def r_u_k(g):
                dve.wait_ge(r_ready, g + 1)
                dve.wait_ge(k_ready, g + 1)
                wait_last(dve, bonus_psum, g)
                for c in range(CH):
                    last = nc.vector.scalar_tensor_tensor(ruk[:, c], half(PROJ_BANK["r"], c), vcol("u", c), kq[:, c],
                                                          ALU.mult, ALU.mult)
                last.then_inc(ruk_ready, 1)

            def diagonal(g):
                dve.wait_ge(bonus_copied, g + 1)
                wait_last(dve, o_psum, 2 * g)
                n = J * CH * 2
                nc.vector.tensor_tensor(A[:].rearrange("p a e t -> p (a e) t"),
                                        ident[:].rearrange("p (a t) -> p a t", a=1).to_broadcast([P, n, Q]),
                                        bonus[:].rearrange("p a (e t) -> p (a e) t", t=1).to_broadcast([P, n, Q]),
                                        ALU.mult).then_inc(diag_written, 1)

            def level(g, n, x_round=None):
                Ln = LEVELS[n]
                nb = TG // (2 * Ln)
                dve.wait_ge(level_psum, 7 * g + n + 1)
                if n == 0:
                    dve.wait_ge(w_ready, g + 1)
                else:
                    dve.wait_ge(wprod, 7 * g + n)
                    dve.wait_ge(q_scaled, 7 * g + n)
                w4 = wdec[n][:].rearrange("p c (b e) -> p c b e", e=2)
                for e in range(2):
                    lo, hi = e * HS, (e + 1) * HS
                    qq = rq[lo:hi, :, e].rearrange("p c (b e l) -> p c b e l", e=2, l=Ln)[:, :, :, 1]
                    last = nc.vector.tensor_tensor(qq, qq, w4[lo:hi, :, :, 0:1].to_broadcast([HS, CH, nb, Ln]), ALU.mult)
                last.then_inc(q_scaled, 1)
                if n > 0:
                    dve.wait_ge(A_copied, 7 * g + n)
                nc.vector.tensor_tensor(wdec[n + 1][:], w4[:, :, :, 0], w4[:, :, :, 1], ALU.mult).then_inc(wprod, 1)
                if n == 0:
                    diagonal(g)
                    dve.wait_ge(diag_written, g + 1)
                    if x_round is not None:
                        x_low(x_round)
                m0 = HALF * n
                nbq = Q // (2 * Ln)
                m = J * CH * 2
                nc.vector.copy_predicated(
                    A[:].rearrange("p a e (b h l) -> p (a e) b h l", h=2, l=Ln)[:, :, :, 1],
                    masks[:, m0:m0 + HALF].bitcast(U32).rearrange("p (a b l) -> p a b l", a=1, l=Ln).to_broadcast(
                        [P, m, nbq, Ln]),
                    bank[LEVEL_BANK[n % 2]][:].rearrange("p (a b l) -> p a b l", a=m, l=Ln)).then_inc(A_copied, 1)

            def state(g, j):
                dve.wait_ge(st_psum, 2 * g + j + 1)
                dve.wait_ge(o_psum, 2 * g + j + 1)
                wait_last(dve, S_ready, 2 * g + j)
                dve.wait_ge(wprod, 7 * g + 7)
                for c in range(CH):
                    for e in range(2):
                        lo, hi = e * HS, (e + 1) * HS
                        last = nc.vector.scalar_tensor_tensor(
                            S[lo:hi, c, lo:hi], S[lo:hi, c, lo:hi], wdec[7][lo:hi, c, j:j + 1],
                            bank[STATE_BANK[j]][lo:hi, c * P + lo:c * P + hi], ALU.mult, ALU.add)
                last.then_inc(S_ready, 1)

            def moments(g, stat, m, n, eps, parts_done, var_ready):
                nc.vector.tensor_tensor(m["sum"][:], stat[:, :, 1], stat[:, :, 4], ALU.add)
                nc.vector.tensor_tensor(m["diff"][:], stat[:, :, 1], stat[:, :, 4], ALU.subtract)
                nc.vector.tensor_tensor(m["m2"][:], stat[:, :, 2], stat[:, :, 5], ALU.add).then_inc(parts_done, 1)
                dve.wait_ge(parts_done, 2 * g + 1)
                nc.vector.tensor_scalar(m["mean"][:], m["sum"][:], 0.5, None, ALU.mult)
                nc.vector.scalar_tensor_tensor(m["sq"][:], m["diff"][:], 0.25, m["diff"][:], ALU.mult, ALU.mult)
                nc.vector.tensor_scalar(m["m2n"][:], m["m2"][:], 1.0 / n, eps, ALU.mult,
                                        ALU.add).then_inc(parts_done, 1)
                dve.wait_ge(parts_done, 2 * g + 2)
                nc.vector.tensor_tensor(m["var"][:], m["sq"][:], m["m2n"][:], ALU.add).then_inc(var_ready, 1)

            def group_norm(g):
                dve.wait_ge(o_psum, 2 * g + 2)
                for j in range(J):
                    for hh in range(HEADS):
                        last = nc.vector.bn_stats(gstat[:, j * HEADS + hh],
                                                  bank[OUT_BANK][:, j * C + hh * HS:j * C + (hh + 1) * HS])
                last.then_inc(gstat_done, 1)
                dve.wait_ge(gstat_done, g + 1)
                wait_last(dve, grs_ready, g)
                moments(g, gstat, gm, HS, GN_EPS, gmv_done, gvar_ready)

            def group_norm_apply(g):
                dve.wait_ge(grs_ready, g + 1)
                wait_last(dve, nT_psum, g)
                for a in range(J * HEADS):
                    j, hh = divmod(a, HEADS)
                    last = nc.vector.tensor_scalar(norm[:, j, hh * HS:(hh + 1) * HS],
                                                   bank[OUT_BANK][:, j * C + hh * HS:j * C + (hh + 1) * HS], gm["mean"][:, a:a + 1],
                                                   grs[:, a:a + 1], ALU.subtract, ALU.mult)
                last.then_inc(norm_ready, 1)

            def residual1(g):
                dve.wait_ge(wo_psum, g + 1)
                wait_last(dve, y_ready, g)
                dve.wait_ge(xtok_loaded, 16 * g + 16)
                nc.vector.tensor_tensor(res[:], halves(WO_BANK), xtok[:], ALU.add).then_inc(res_ready, 1)
                dve.wait_ge(res_ready, g + 1)
                for j in range(J):
                    last = nc.vector.bn_stats(stat1[:, j], res[:, j])
                last.then_inc(stat1_done, 1)
                dve.wait_ge(stat1_done, g + 1)
                moments(g, stat1, m1, C, LN_EPS, mv1_done, var1_ready)

            def norm1(g):
                dve.wait_ge(rs1_ready, g + 1)
                dve.wait_ge(yT_psum, g + 1)
                dve.wait_ge(res2_ready, g + 1)
                for j in range(J):
                    last = nc.vector.tensor_scalar(y[:, j], res[:, j], m1["mean"][:, j:j + 1], rs1[:, j:j + 1], ALU.subtract,
                                                   ALU.mult)
                last.then_inc(y_ready, 1)

            def split_low():
                dve.wait_ge(whi_ready, 1)
                nc.vector.tensor_tensor(wu[1][:], wup[:], wu[0][:].bitcast(F32), ALU.subtract).then_inc(wu_lo_ready, 1)

            def rotate_down():
                dve.wait_ge(L["wdown"], 16)
                bufs = [wdown, wd_tmp, wdown, wd_tmp]
                for s, dist in enumerate((4, 2, 1)):
                    a = bufs[s][:].rearrange("p (b e l) c -> p b e (l c)", e=2, l=dist)
                    o = bufs[s + 1][:].rearrange("p (b e l) c -> p b e (l c)", e=2, l=dist)
                    if s:
                        dve.wait_ge(wd_step, s)
                    nc.vector.tensor_tensor(o[:, :, 0], a[:, :, 0], a[:, :, 1], ALU.add)
                    nc.vector.tensor_tensor(o[:, :, 1], a[:, :, 0], a[:, :, 1], ALU.subtract).then_inc(wd_step, 1)

            def scale_down(i):
                if i == 0:
                    dve.wait_ge(L["wsrow"], 16)
                dve.wait_ge(wd_psum, i + 1)
                for e in range(2):
                    it = 2 * i + e
                    last = nc.vector.scalar_tensor_tensor(wdown[:, it], half(WD_BANK, e), sdu[:, it:it + 1], wsrow[:],
                                                          ALU.mult, ALU.mult)
                last.then_inc(wd_ready, 1)

            def y_butterfly(r):
                dve.wait_ge(ya_ready, r + 1)
                dve.wait_ge(xh_psum, r)
                nc.vector.scalar_tensor_tensor(yu[:, 0], half(FFN_BANK, 1), vcol("su_ug", 1), ya[:], ALU.mult, ALU.add)
                nc.vector.scalar_tensor_tensor(yu[:, 1], half(FFN_BANK, 1), vcol("su_ug", 1), ya[:], ALU.mult,
                                               ALU.subtract).then_inc(yu_ready, 1)

            def x_low(r):
                dve.wait_ge(xh_ready, r + 1)
                dve.wait_ge(ug_psum, IT * r)
                s = 1.0 / (C ** 0.5 * FFN_SCALE)
                for c in range(CH):
                    last = nc.vector.scalar_tensor_tensor(xh[1][:, c], half(FFN_BANK, c), -s if c else s,
                                                          xh[0][:, c].bitcast(F32), ALU.mult, ALU.subtract)
                last.then_inc(xl_ready, 1)

            def swiglu(r, it):
                dve.wait_ge(silu_ready, IT * r + it + 1)
                if it == 0:
                    dve.wait_ge(dn_psum, r)
                nc.vector.scalar_tensor_tensor(h[:, it], half(UG_BANK[it % 2], 0), wsu[:, it:it + 1], sg[:, it % 2],
                                               ALU.mult, ALU.mult).then_inc(h_ready, 1)

            def residual2(r):
                dve.wait_ge(dn_psum, r + 1)
                dve.wait_ge(out_ready, r)
                dve.wait_ge(y_ready, r)
                nc.vector.tensor_tensor(res2[:], halves(FFN_BANK), y[:], ALU.add).then_inc(res2_ready, 1)
                dve.wait_ge(res2_ready, r + 1)
                for j in range(J):
                    last = nc.vector.bn_stats(stat2[:, j], res2[:, j])
                last.then_inc(stat2_done, 1)
                dve.wait_ge(stat2_done, r)
                moments(r - 1, stat2, m2, C, LN_EPS, mv2_done, var2_ready)

            def norm2(r):
                dve.wait_ge(rs2_ready, r + 1)
                dve.wait_ge(stored, 16 * r)
                for j in range(J):
                    last = nc.vector.tensor_scalar(outs[:, j], res2[:, j], m2["mean"][:, j:j + 1], rs2[:, j:j + 1],
                                                   ALU.subtract, ALU.mult)
                last.then_inc(out_ready, 1)

            def turn(g, first=False, last=False):
                if first:
                    token_mix(1)
                for n in range(7):
                    level(g, n, x_round=g if n == 0 and not first else None)
                    if first:
                        if 1 <= n <= 5:
                            mix(1, n - 1)
                        if 1 <= n <= 4:
                            scale_down(n - 1)
                    elif n > 0:
                        swiglu(g, n - 1)
                if not first:
                    swiglu(g, 6)
                    swiglu(g, 7)
                state(g, 0)
                if last:
                    group_norm(g)
                    group_norm_apply(g)
                    residual2(g)
                    residual1(g)
                    norm2(g)
                    norm1(g)
                    y_butterfly(g + 1)
                    return
                if not first:
                    token_mix(g + 1)
                    residual2(g)
                state(g, 1)
                group_norm(g)
                if not first:
                    mix(g + 1, 0)
                    mix(g + 1, 1)
                group_norm_apply(g)
                if first:
                    split_low()
                else:
                    norm2(g)
                if not first:
                    for i in range(2, 5):
                        mix(g + 1, i)
                residual1(g)
                r_u_k(g + 1)
                norm1(g)
                y_butterfly(g + 1)

            dve.wait_ge(L["vec"], 16)
            nc.vector.tensor_scalar(wsu[:], vec[:, VEC["ws_up"]:VEC["ws_up"] + 2 * IT], FFN_SCALE, None, ALU.mult)
            nc.vector.tensor_scalar(sdu[:], vec[:, VEC["su_dp"]:VEC["su_dp"] + IT],
                                    1.0 / INTER ** 0.5, None, ALU.mult).then_inc(scales_ready, 1)
            dve.wait_ge(scales_ready, 1)
            dve.wait_ge(zeroed, 1)
            token_mix(0)
            for i in range(5):
                mix(0, i)
            rotate_down()
            r_u_k(0)
            dve.wait_ge(L["const"], 32)
            dve.wait_ge(L["masks"], 16)
            turn(0, first=True)
            with dve.Fori(1, G - 1) as g:
                turn(g)
            turn(G - 1, last=True)
            x_low(G)
            for it in range(IT):
                swiglu(G, it)
            residual2(G)
            norm2(G)

        @block.tensor
        def _(pe):
            def loaded(name, count=16):
                pe.wait_ge(L[name], count)

            def z(g):
                pe.wait_ge(xxx_ready, g + 1)
                if isinstance(g, int) and g == 1:
                    pe.wait_ge(v_ready, 1)
                elif not isinstance(g, int):
                    pe.wait_ge(h_ready, IT * g)
                for c in range(CH):
                    nc.tensor.matmul(half(Z_BANK, 0), w1[:, c, 0:P], xxx[:, c], start=c == 0, stop=c == CH - 1)
                for c in range(CH):
                    last = nc.tensor.matmul(bank[Z_BANK][0:DMIX, TG:2 * TG], w1[:, c, P:P + DMIX], xxx[:, c],
                                            start=c == 0, stop=c == CH - 1)
                last.then_inc(z_psum, 1)

            def mix(g, i, early=False):
                n = MIXES[i]
                f = PART[n]
                if i == 0:
                    pe.wait_ge(z_tanh, g + 1)
                    if early:
                        pe.wait_ge(g_ready, 1)
                elif n == "k" and not early:
                    wait_last(pe, kT_ready, g)
                elif n == "r":
                    if early:
                        pe.wait_ge(bonus_copied, 1)
                    else:
                        wait_last(pe, S_ready, 2 * g)
                elif n == "v":
                    wait_last(pe, res2_ready, g)
                lo, hi = (0, DMIX) if n == "g" else (f * DMIX, (f + 1) * DMIX)
                for c in range(CH):
                    w, zz = (w2g, ztg) if n == "g" else (w2, zt)
                    last = nc.tensor.matmul(half(MIX_BANK[n], c), w[lo:hi, c * P:(c + 1) * P], zz[lo:hi, :], start=True,
                                            stop=True, tile_position=(lo, 0))
                last.then_inc(mix_psum, 1)

            def dec1(g):
                pe.wait_ge(xm_ready, 5 * g + 1)
                for c in range(CH):
                    last = nc.tensor.matmul(bank[DEC1_BANK][0:DDEC, 0:TG], dw1[:, c], xm["w"][:, c], start=c == 0,
                                            stop=c == CH - 1)
                last.then_inc(dec1_psum, 1)

            def dec2(g):
                pe.wait_ge(dec1_tanh, g + 1)
                pe.wait_ge(mixed_ready, 5 * g + 3)
                for c in range(CH):
                    last = nc.tensor.matmul(half(DEC2_BANK, c), dw2[:, c * P:(c + 1) * P], tdec[:], start=True, stop=True)
                last.then_inc(dec2_psum, 1)

            def channels(g, n, done):
                i = MIXES.index(n)
                pe.wait_ge(xm_ready, 5 * g + i + 1)
                if n == "r":
                    wait_last(pe, S_ready, 2 * g)
                for a in range(CH):
                    for c in range(CH):
                        last = nc.tensor.matmul(half(PROJ_BANK[n], a), proj[n][:, c, a * P:(a + 1) * P], xm[n][:, c],
                                                start=c == 0, stop=c == CH - 1)
                last.then_inc(done, 1)

            def v(g):
                pe.wait_ge(xm_ready, 5 * g + 4)
                pe.wait_ge(mixed_ready, 5 * g + 5)
                for j in range(J):
                    for c in range(CH):
                        last = nc.tensor.matmul(half(PROJ_BANK["v"], j), xm["v"][:, c, j * Q:(j + 1) * Q],
                                                proj["v"][:, c], start=c == 0, stop=c == CH - 1)
                last.then_inc(v_psum, 1)

            def diagonal(g):
                pe.wait_ge(ruk_ready, g + 1)
                pe.wait_ge(w_ready, g + 1)
                for a in range(J * CH):
                    j, c = divmod(a, CH)
                    last = nc.tensor.matmul(bank[DIAG_BANK][:, 2 * a:2 * a + 2], ruk[:, c, j * Q:(j + 1) * Q], heads[:],
                                            start=True, stop=True)
                last.then_inc(bonus_psum, 1)

            def level(g, n):
                Ln = LEVELS[n]
                if n == 0:
                    pe.wait_ge(k_ready, g + 1)
                    pe.wait_ge(r_ready, g + 1)
                    wait_last(pe, nT_ready, g)
                elif n == 1:
                    pe.wait_ge(q_scaled, 7 * g + 1)
                    pe.wait_ge(k_scaled, 7 * g + 1)
                    pe.wait_ge(ruk_ready, g + 1)
                else:
                    pe.wait_ge(q_scaled, 7 * g + n)
                    pe.wait_ge(k_scaled, 7 * g + n)
                    pe.wait_ge(A_copied, 7 * g + n - 1)
                for a in range(J * CH):
                    j, c = divmod(a, CH)
                    qq = rq[:, c, :, j * Q:(j + 1) * Q].rearrange("p e (b h l) -> p e b h l", h=2, l=Ln)[:, :, :, 1]
                    last = nc.tensor.matmul(
                        bank[LEVEL_BANK[n % 2]][:, a * Q:(a + 1) * Q].rearrange("p (e b l) -> p e b l", e=2, l=Ln),
                        kq[:, c, j * Q:(j + 1) * Q], qq, start=True, stop=True)
                last.then_inc(level_psum, 1)

            def k_transpose(g, first):
                pe.wait_ge(k_scaled, 7 * g + 7)
                if first:
                    pe.wait_ge(mixed_ready, 5 + 2)
                for a in range(J * CH):
                    j, c = divmod(a, CH)
                    last = nc.tensor.transpose(bank[KT_BANK][:, a * P:(a + 1) * P], kq[:, c, j * Q:(j + 1) * Q], ident[:])
                last.then_inc(kT_psum, 1)

            def chunk(g, j, first):
                if j == 0:
                    if first:
                        pe.wait_ge(wd_ready, IT // 2)
                    pe.wait_ge(A_copied, 7 * g + 7)
                    pe.wait_ge(q_scaled, 7 * g + 7)
                    pe.wait_ge(v_ready, g + 1)
                    wait_last(pe, res_ready, g)
                wait_last(pe, S_ready, 2 * g + j)
                for c in range(CH):
                    at = j * C + c * P
                    for e in range(2):
                        nc.tensor.matmul(bank[OUT_BANK][:, at + e * HS:at + (e + 1) * HS], rq[:, c, e, j * Q:(j + 1) * Q],
                                         S[:, c, e * HS:(e + 1) * HS], start=True, stop=False)
                        last = nc.tensor.matmul(bank[OUT_BANK][:, at + e * HS:at + (e + 1) * HS], A[:, j * CH + c, e],
                                                vs[:, j, c * P + e * HS:c * P + (e + 1) * HS], start=False, stop=True)
                last.then_inc(o_psum, 1)
                if j == 0:
                    pe.wait_ge(kT_ready, g + 1)
                    pe.wait_ge(bonus_copied, g + 1)
                    if first:
                        pe.wait_ge(mixed_ready, 5 + 3)
                for c in range(CH):
                    last = nc.tensor.matmul(bank[STATE_BANK[j]][:, c * P:(c + 1) * P], kT[:, j, c],
                                            vs[:, j, c * P:(c + 1) * P], start=True, stop=True)
                last.then_inc(st_psum, 1)

            def norm_transpose(g):
                pe.wait_ge(norm_ready, g + 1)
                for c in range(CH):
                    for j in range(J):
                        last = nc.tensor.transpose(bank[NT_BANK][:, c * TG + j * Q:c * TG + (j + 1) * Q],
                                                   norm[:, j, c * P:(c + 1) * P], ident[:])
                last.then_inc(nT_psum, 1)

            def w_o(g):
                pe.wait_ge(og_ready, g + 1)
                for j in range(J):
                    for c in range(CH):
                        last = nc.tensor.matmul(half(WO_BANK, j), og[:, c, j * Q:(j + 1) * Q], proj["o"][:, c],
                                                start=c == 0, stop=c == CH - 1)
                last.then_inc(wo_psum, 1)

            def rotate_down(i):
                if i == 0:
                    loaded("const", 32)
                    pe.wait_ge(wd_step, 3)
                else:
                    pe.wait_ge(wd_ready, i)
                nc.tensor.matmul(bank[WD_BANK][:], had[:], wd_tmp[:, 2 * i:2 * i + 2].rearrange("p a c -> p (a c)"),
                                 start=True, stop=True).then_inc(wd_psum, 1)

            def y_transpose(r, last):
                pe.wait_ge(y_ready, r)
                if not last:
                    pe.wait_ge(mixed_ready, 5 * r + 4)
                pe.wait_ge(res2_ready, r)
                for c in range(CH):
                    for j in range(J):
                        last = nc.tensor.transpose(bank[FFN_BANK][:, c * TG + j * Q:c * TG + (j + 1) * Q],
                                                   y[:, j, c * P:(c + 1) * P], ident[:])
                last.then_inc(yT_psum, 1)

            def rotate_x(r):
                pe.wait_ge(yu_ready, r + 1)
                nc.tensor.matmul(bank[FFN_BANK][:], had[:], yu[:].rearrange("p c t -> p (c t)"), start=True,
                                 stop=True).then_inc(xh_psum, 1)

            def up_gate(r, it):
                if it == 0:
                    pe.wait_ge(xl_ready, r + 1)
                    if not isinstance(r, int) or r < G:
                        pe.wait_ge(v_ready, r + 1)
                        pe.wait_ge(g_ready, r + 1)
                pe.wait_ge(h_ready, IT * r + max(it - 1, 0))
                b = UG_BANK[it % 2]
                for e, w in enumerate((wu, wg)):
                    terms = [(c, wp, xp) for c in range(CH) for wp, xp in ((1, 0), (0, 1), (0, 0))]
                    for n, (c, wp, xp) in enumerate(terms):
                        last = nc.tensor.matmul(half(b, e), w[wp][:, c, it * P:(it + 1) * P], xh[xp][:, c], start=n == 0,
                                                stop=n == len(terms) - 1)
                last.then_inc(ug_psum, 1)

            def down(r, j):
                if j == 0:
                    pe.wait_ge(h_ready, IT * r + IT)
                for it in range(IT):
                    last = nc.tensor.matmul(half(FFN_BANK, j), h[:, it, j * Q:(j + 1) * Q], wdown[:, it],
                                            start=it == 0, stop=it == IT - 1)
                if j == J - 1:
                    last.then_inc(dn_psum, 1)

            def turn(g, first=False, last=False):
                diagonal(g)
                for n in range(7):
                    level(g, n)
                    if first:
                        if n == 0:
                            z(1)
                        elif n <= 5:
                            mix(1, n - 1, early=True)
                        else:
                            dec1(1)
                        if 1 <= n <= 4:
                            rotate_down(n - 1)
                    elif n == 0:
                        rotate_x(g)
                    else:
                        up_gate(g, n - 1)
                if not first:
                    up_gate(g, 6)
                k_transpose(g, first)
                if not first:
                    up_gate(g, 7)
                chunk(g, 0, first)
                if last:
                    chunk(g, 1, first)
                    down(g, 0)
                    norm_transpose(g)
                    down(g, 1)
                    w_o(g)
                    y_transpose(g + 1, last)
                    return
                if first:
                    chunk(0, 1, first)
                    channels(1, "k", k_psum)
                    dec2(1)
                    channels(1, "r", r_psum)
                    v(1)
                    norm_transpose(0)
                    channels(1, "g", g_psum)
                    loaded("W_o")
                    w_o(0)
                else:
                    down(g, 0)
                    z(g + 1)
                    down(g, 1)
                    chunk(g, 1, first)
                    for i in range(5):
                        mix(g + 1, i)
                    norm_transpose(g)
                    dec1(g + 1)
                    channels(g + 1, "k", k_psum)
                    dec2(g + 1)
                    w_o(g)
                    channels(g + 1, "r", r_psum)
                    v(g + 1)
                    channels(g + 1, "g", g_psum)
                y_transpose(g + 1, last)

            loaded("w1")
            z(0)
            loaded("w2", 32)
            for i in range(5):
                mix(0, i)
            loaded("dw", 32)
            dec1(0)
            loaded("W_k")
            channels(0, "k", k_psum)
            dec2(0)
            loaded("W_r")
            channels(0, "r", r_psum)
            loaded("W_v")
            v(0)
            loaded("W_g")
            channels(0, "g", g_psum)
            loaded("heads")
            turn(0, first=True)
            pe.wait_ge(wu_lo_ready, 1)
            pe.wait_ge(wg_lo_ready, 1)
            with pe.Fori(1, G - 1) as g:
                turn(g)
            turn(G - 1, last=True)
            rotate_x(G)
            for it in range(IT):
                up_gate(G, it)
            for j in range(J):
                down(G, j)


def _masks(np):
    s = np.arange(Q)[:, None]
    parts = []
    for n in LEVELS:
        t = np.arange(Q)
        t = t[(t // n) % 2 == 1][None, :]
        parts.append((s // (2 * n) == t // (2 * n)) & ((s // n) % 2 == 0))
    return np.concatenate(parts, axis=1).astype(np.float32)


def _hadamard(np):
    m = np.ones((1, 1), np.float32)
    while m.shape[0] < P:
        m = np.block([[m, m], [m, -m]])
    return m


def kernel(**inputs):
    import numpy as np
    import concourse.bacc as _bacc
    from concourse import mybir as _mybir
    from concourse.bass_utils import run_bass_kernel_spmd as _run

    a = {k: np.asarray(v) for k, v in inputs.items()}
    A_, F_ = "L0_attn_", "L0_ffn_"

    def rows(m):
        return m.reshape(-1, P, m.shape[1]).transpose(1, 0, 2)

    def cols(v):
        return v.reshape(-1, P).T

    x = a[A_ + "hidden"][0]
    w2 = a[A_ + "time_maa_w2"]
    vec = [cols(a[A_ + "time_maa_" + n]) for n in "xwkrvg"]
    vec += [cols(a[A_ + n]) for n in ("time_decay", "time_faaaa", "ln_gamma", "ln_beta")]
    vec += [cols(a[F_ + n]) for n in ("SU_ug", "Wscale_ug", "SU_dp")]
    arrays = {
        "xT": rows(x.T), "xtok": rows(x), "vec": np.concatenate(vec, axis=1),
        "w1": rows(a[A_ + "time_maa_w1"]), "w2": w2[0:4].reshape(P, C), "w2g": w2[4],
        "dw1": rows(a[A_ + "time_decay_w1"]), "dw2": a[A_ + "time_decay_w2"],
        "wup": rows(a[F_ + "W_up"].T), "wgate": rows(a[F_ + "W_gate"].T), "wdown": rows(a[F_ + "W_down"].T),
        "wsrow": a[F_ + "Wscale_dp"].reshape(1, C),
        "had": _hadamard(np), "ident": np.eye(P, dtype=np.float32), "masks": _masks(np),
        "heads": np.kron(np.eye(2, dtype=np.float32), np.ones((HS, 1), np.float32)),
    }
    for n in "krvgo":
        arrays["W_" + n] = rows(a[A_ + "W_" + n].T)
    arrays = {k: np.ascontiguousarray(v) for k, v in arrays.items()}

    nc = _bacc.Bacc("TRN2", target_bir_lowering=False, num_devices=1)
    d = {k: nc.dram_tensor(f"{k}_dram", v.shape, _mybir.dt.from_np(v.dtype), kind="ExternalInput").ap()
         for k, v in arrays.items()}
    out = nc.dram_tensor("out_dram", (1, T, C), F32, kind="ExternalOutput").ap()
    d["out"] = out.rearrange("o (j p) c -> p (o j) c", p=P)
    build(nc, d)
    r = _run(nc, [{f"{k}_dram": v for k, v in arrays.items()}], core_ids=[0])
    return r.results[0]["out_dram"]
```

```python
from contextlib import ExitStack

import concourse.bass as bass
from concourse import mybir

F32 = mybir.dt.float32
F32R = mybir.dt.float32r
U32 = mybir.dt.uint32
ACT = mybir.ActivationFunctionType
ALU = mybir.AluOpType

T = 1024
C = 256
P = 128
CH = C // P
HS = 64
HEADS = C // HS
TG = 256
G = T // TG
Q = 128
J = TG // Q
DMIX = 32
DDEC = 64
INTER = 1024
IT = INTER // P
LEVELS = [1, 2, 4, 8, 16, 32, 64]
HALF = Q // 2
FFN_SCALE = 64.0
GN_EPS = 1e-05 * 8.0 ** 2
LN_EPS = 1e-05

VEC = {}
_at = 0
for _name, _n in [("maa_x", CH), ("maa_w", CH), ("maa_k", CH), ("maa_r", CH), ("maa_v", CH), ("maa_g", CH),
                  ("decay", CH), ("u", CH), ("gamma", CH), ("beta", CH), ("su_ug", CH), ("ws_up", IT),
                  ("ws_gate", IT), ("su_dp", IT)]:
    VEC[_name] = _at
    _at += _n
VCOLS = _at

CONST = {}
_at = 0
for _name, _n in [("had", P), ("had_neg", P), ("ident", P), ("heads", 2), ("masks", HALF * len(LEVELS))]:
    CONST[_name] = (_at, _at + _n)
    _at += _n
CCOLS = _at

PART = {"w": 0, "k": 1, "v": 2, "r": 3, "g": 4}
MIXES = ["w", "k", "r", "v", "g"]
Z_BANK = 5
MIX_BANK = {"w": 6, "k": 1, "r": 0, "v": 7, "g": 5}
DEC1_BANK = 6
DEC2_BANK = 0
PROJ_BANK = {"k": 1, "r": 4, "v": 5, "g": 6}
LEVEL_BANK = [3, 4]
DIAG_BANK = 0
KT_BANK = 1
OUT_BANK = 2
STATE_BANK = [0, 4]
NT_BANK = 3
WO_BANK = 2
UG_BANK = [5, 6]
WD_BANK = [2, 7]
FFN_BANK = 7
DOWN_AT = [0, 5]
HB = 4
LAST_BANK = [7, 2]


def wait_last(eng, sem, value):
    if not isinstance(value, int) or value > 0:
        eng.wait_ge(sem, value)


def build(nc, d):
    with ExitStack() as ctx:
        def sb(name, shape, dt=F32):
            return ctx.enter_context(nc.sbuf_tensor(name, shape, dt))

        def sem(name):
            return ctx.enter_context(nc.semaphore(name))

        def moment_tiles(name, n):
            return {k: sb(f"{name}_{k}", [P, n]) for k in ("sum", "diff", "m2", "sq", "mean", "var", "m2n")}

        bank = [ctx.enter_context(nc.psum_tensor(f"bank{i}", [P, 512], F32)) for i in range(8)]

        xT = sb("xT", [P, CH, TG + 1])
        xtok = sb("xtok", [P, J, C])
        vec = sb("vec", [P, VCOLS])
        w1 = sb("w1", [P, CH, 5 * DMIX])
        w2 = sb("w2", [P, C])
        w2g = sb("w2g", [DMIX, C])
        dw1 = sb("dw1", [P, CH, DDEC])
        dw2 = sb("dw2", [DDEC, C])
        proj = {n: sb(f"W_{n}", [P, CH, C]) for n in "krvgo"}
        wup = sb("wup", [P, CH, INTER])
        wgate = sb("wgate", [P, CH, INTER])
        wdownT = sb("wdownT", [P, IT, C])
        wdown = sb("wdown", [P, IT, C])
        wsrow = sb("wsrow", [P, C])
        const = sb("const", [P, CCOLS])
        had, had_neg, ident, heads, masks = (const[:, CONST[n][0]:CONST[n][1]] for n in CONST)
        neghalf = sb("neghalf", [P, J * HEADS])

        xx = sb("xx", [P, CH, TG])
        xxx = sb("xxx", [P, CH, TG])
        mixed = sb("mixed", [P, 2, CH, TG])
        xm = {n: sb(f"x_{n}", [P, CH, TG]) for n in MIXES}
        zt = sb("zt", [P, TG])
        ztg = sb("ztg", [DMIX, TG])
        tdec = sb("tdec", [DDEC, TG])
        edec = sb("edec", [P, CH, TG])
        wdec = [sb(f"wdec{L}", [P, CH, TG // L]) for L in LEVELS + [Q]]
        kq = sb("kq", [P, CH, TG])
        rq = sb("rq", [P, CH, 2, TG])
        ruk = sb("ruk", [P, CH, TG])
        bonus = sb("bonus", [P, J * CH, 2])
        vs = sb("vs", [P, J, C])
        gT = sb("gT", [P, CH, TG])
        A = sb("A", [P, J * CH, 2, Q])
        kT = sb("kT", [P, J, CH, P])
        S = sb("S", [P, CH, P])
        gstat = sb("gstat", [P, J * HEADS, 6])
        gm = moment_tiles("gm", J * HEADS)
        grs = sb("grs", [P, J * HEADS])
        norm = sb("norm", [P, J, C])
        nT = sb("nT", [P, CH, TG])
        og = sb("og", [P, CH, TG])
        res = sb("res", [P, J, C])
        stat1 = sb("stat1", [P, J, 6])
        m1 = moment_tiles("m1", J)
        rs1 = sb("rs1", [P, J])
        y = sb("y", [P, J, C])

        wsu = sb("wsu", [P, 2 * IT])
        sdu = sb("sdu", [P, IT])
        ya = sb("ya", [P, TG])
        yu = sb("yu", [P, CH, TG])
        xh = [sb(f"xh_{n}", [P, CH, TG], F32R) for n in ("hi", "lo")]
        wu = [sb(f"wu_{n}", [P, CH, INTER], F32R) for n in ("hi", "lo")]
        wg = [sb(f"wg_{n}", [P, CH, INTER], F32R) for n in ("hi", "lo")]
        sg = sb("sg", [P, 2, TG])
        h = sb("h", [P, HB, TG])
        hs = [sb(f"h_{n}", [P, IT, TG], F32R) for n in ("hi", "lo")]
        wd = [sb(f"wd_{n}", [P, IT, C], F32R) for n in ("hi", "lo")]
        res2 = sb("res2", [P, J, C])
        stat2 = sb("stat2", [P, J, 6])
        m2 = moment_tiles("m2", J)
        rs2 = sb("rs2", [P, J])
        outs = sb("outs", [P, J, C])

        L = {n: sem(f"load_{n}") for n in ("vec", "w1", "w2", "dw", "W_k", "W_r", "W_v", "W_g", "W_o", "wup",
                                          "wgate", "wdown", "wsrow", "const")}
        warm_operand = sem("warm_operand")
        zeroed = sem("zeroed")
        tanh_loaded = sem("tanh_loaded")
        xT_loaded = sem("xT_loaded")
        xtok_loaded = sem("xtok_loaded")
        xxx_ready = sem("xxx_ready")
        z_psum = sem("z_psum")
        z_tanh = sem("z_tanh")
        mix_psum = sem("mix_psum")
        mixed_ready = sem("mixed_ready")
        xm_ready = sem("xm_ready")
        dec1_psum = sem("dec1_psum")
        dec1_tanh = sem("dec1_tanh")
        dec2_psum = sem("dec2_psum")
        exp_ready = sem("exp_ready")
        w_ready = sem("w_ready")
        k_psum = sem("k_psum")
        r_psum = sem("r_psum")
        v_psum = sem("v_psum")
        g_psum = sem("g_psum")
        k_ready = sem("k_ready")
        r_ready = sem("r_ready")
        v_ready = sem("v_ready")
        g_ready = sem("g_ready")
        level_psum = sem("level_psum")
        q_scaled = sem("q_scaled")
        k_scaled = sem("k_scaled")
        wprod = sem("wprod")
        ruk_ready = sem("ruk_ready")
        bonus_psum = sem("bonus_psum")
        bonus_copied = sem("bonus_copied")
        diag_written = sem("diag_written")
        A_copied = sem("A_copied")
        kT_psum = sem("kT_psum")
        kT_ready = sem("kT_ready")
        o_psum = sem("o_psum")
        st_psum = sem("st_psum")
        S_ready = sem("S_ready")
        gvar_ready = sem("gvar_ready")
        grs_ready = sem("grs_ready")
        norm_ready = sem("norm_ready")
        nT_psum = sem("nT_psum")
        nT_ready = sem("nT_ready")
        og_ready = sem("og_ready")
        wo_psum = sem("wo_psum")
        res_ready = sem("res_ready")
        var1_ready = sem("var1_ready")
        rs1_ready = sem("rs1_ready")
        y_ready = sem("y_ready")
        scales_ready = sem("scales_ready")
        wd_step = sem("wd_step")
        wd_psum = sem("wd_psum")
        wd_ready = sem("wd_ready")
        yT_psum = sem("yT_psum")
        ya_ready = sem("ya_ready")
        yu_ready = sem("yu_ready")
        xh_psum = sem("xh_psum")
        xh_ready = sem("xh_ready")
        xl_ready = sem("xl_ready")
        whi_ready = sem("whi_ready")
        wd_hi_ready = sem("wd_hi_ready")
        wd_lo_ready = sem("wd_lo_ready")
        wu_lo_ready = sem("wu_lo_ready")
        wg_lo_ready = sem("wg_lo_ready")
        ug_psum = sem("ug_psum")
        silu_ready = sem("silu_ready")
        h_ready = sem("h_ready")
        hh_ready = sem("hh_ready")
        hl_ready = sem("hl_ready")
        dn_psum = sem("dn_psum")
        res2_ready = sem("res2_ready")
        var2_ready = sem("var2_ready")
        rs2_ready = sem("rs2_ready")
        out_ready = sem("out_ready")
        stored = sem("stored")
        xx_done = sem("xx_done")
        gstat_done = sem("gstat_done")
        gmv_done = sem("gmv_done")
        centred = sem("centred")
        stat1_done = sem("stat1_done")
        mv1_done = sem("mv1_done")
        stat2_done = sem("stat2_done")
        mv2_done = sem("mv2_done")

        def vcol(name, i, lo=0, hi=P):
            return vec[lo:hi, VEC[name] + i:VEC[name] + i + 1]

        now, before = xT[:, :, 1:TG + 1], xT[:, :, 0:TG]

        def flat(t):
            return t[:].rearrange("p c t -> p (c t)")

        def half(b, c):
            return bank[b][:, c * TG:(c + 1) * TG]

        def halves(b):
            return bank[b][:, :].rearrange("p (c t) -> p c t", c=2)

        block = ctx.enter_context(nc.Block())

        @block.sync
        def _(sp):
            sp.dma_start(now, d["xT"][:, :, 0:TG]).then_inc(xT_loaded, 16)
            sp.dma_start(w1[:], d["w1"]).then_inc(L["w1"], 16)
            sp.dma_start(dw1[:], d["dw1"]).then_inc(L["dw"], 16)
            for n in "krvg":
                sp.dma_start(proj[n][:], d["W_" + n]).then_inc(L["W_" + n], 16)
            sp.dma_start(wdownT[:], d["wdown"]).then_inc(L["wdown"], 16)
            sp.dma_start(const[:], d["const"]).then_inc(L["const"], 16)

            def load_xT(g):
                wait_last(sp, xm_ready, 5 * g)
                sp.dma_start(xT[:], d["xT"][:, :, bass.ds(g * TG - 1, TG + 1)]).then_inc(xT_loaded, 16)

            def load_xtok(g):
                wait_last(sp, y_ready, g)
                sp.dma_start(xtok[:], d["xtok"][:, bass.ds(g * J, J), :]).then_inc(xtok_loaded, 16)

            def store(g):
                sp.wait_ge(out_ready, g + 2)
                sp.dma_start(d["out"][:, bass.ds(g * J, J), :], outs[:]).then_inc(stored, 16)

            load_xT(1)
            sp.dma_start(wsrow[:], d["wsrow"].to_broadcast([P, C])).then_inc(L["wsrow"], 16)
            sp.dma_start(wup[:], d["wup"]).then_inc(L["wup"], 16)
            sp.dma_start(wgate[:], d["wgate"]).then_inc(L["wgate"], 16)
            sp.dma_start(proj["o"][:], d["W_o"]).then_inc(L["W_o"], 16)
            sp.dma_start(xtok[:], d["xtok"][:, 0:J, :]).then_inc(xtok_loaded, 16)
            load_xtok(1)
            load_xT(2)
            with sp.Fori(1, G - 2) as g:
                load_xT(g + 2)
                store(g - 1)
                load_xtok(g + 1)
            store(G - 3)
            load_xtok(G - 1)
            store(G - 2)
            for j in range(J):
                sp.wait_ge(out_ready, G + 1 + j)
                sp.dma_start(d["out"][:, (G - 1) * J + j, :], outs[:, j]).then_inc(stored, 16)
            sp.wait_ge(stored, 16 * (G + J))

        @block.gpsimd
        def _(pool):
            nc.gpsimd.memset(xm["w"][:], 0.0).then_inc(warm_operand, 1)
            nc.gpsimd.memset(S[:], 0.0)
            nc.gpsimd.memset(xT[:, :, 0:1], 0.0)
            nc.gpsimd.memset(neghalf[:], -0.5)
            nc.gpsimd.memset(rq[:], 0.0).then_inc(zeroed, 1)
            pool.wait_ge(zeroed, 1)
            for s, n in [(yT_psum, 1), (ya_ready, 1), (yu_ready, 1), (xh_psum, 1), (xh_ready, 1), (xl_ready, 1),
                         (ug_psum, IT), (silu_ready, IT), (h_ready, IT), (hh_ready, IT), (hl_ready, IT),
                         (dn_psum, 1), (res2_ready, 1), (var2_ready, 1),
                         (rs2_ready, 1), (out_ready, 1), (stored, 16)]:
                pool.sem_inc(s, n)

            def mix_add(g, i):
                pool.wait_ge(mixed_ready, 5 * g + i + 1)
                wait_last(pool, {"w": dec1_psum, "k": k_psum, "r": r_psum, "v": v_psum, "g": g_psum}[MIXES[i]], g)
                nc.gpsimd.tensor_tensor(xm[MIXES[i]][:], mixed[:, i % 2], now, ALU.add).then_inc(xm_ready, 1)

            def scale_k(g, n):
                Ln = LEVELS[n]
                pool.wait_ge(level_psum, 7 * g + n + 1)
                if n == 0:
                    pool.wait_ge(w_ready, g + 1)
                else:
                    pool.wait_ge(wprod, 7 * g + n)
                    pool.wait_ge(k_scaled, 7 * g + n)
                kk = kq[:].rearrange("p c (b e l) -> p (c b) e l", e=2, l=Ln)[:, :, 0]
                ww = wdec[n][:].rearrange("p c (b e) -> p (c b) e", e=2)[:, :, 1:2].to_broadcast([P, CH * TG // (2 * Ln), Ln])
                nc.gpsimd.tensor_tensor(kk, kk, ww, ALU.mult).then_inc(k_scaled, 1)

            def group_rsqrt(g):
                pool.wait_ge(gvar_ready, g + 1)
                wait_last(pool, norm_ready, g)
                nc.gpsimd.tensor_tensor(grs[:], gm["var"][:], neghalf[:], ALU.pow).then_inc(grs_ready, 1)

            def rsqrt1(g):
                pool.wait_ge(var1_ready, g + 1)
                wait_last(pool, y_ready, g)
                nc.gpsimd.tensor_tensor(rs1[:], m1["var"][:], neghalf[:, 0:J], ALU.pow).then_inc(rs1_ready, 1)

            def rsqrt2(r):
                pool.wait_ge(var2_ready, r + 1)
                pool.wait_ge(out_ready, r)
                nc.gpsimd.tensor_tensor(rs2[:], m2["var"][:], neghalf[:, 0:J], ALU.pow).then_inc(rs2_ready, 1)

            def split_low(parts, w, high_ready, highs, done, lo=0, hi=None):
                pool.wait_ge(high_ready, highs)
                nc.gpsimd.tensor_tensor(parts[1][:, lo:hi], w[:, lo:hi], parts[0][:, lo:hi].bitcast(F32),
                                        ALU.subtract).then_inc(done, 1)

            def h_low(r, it):
                pool.wait_ge(hh_ready, IT * r + it + 1)
                if it == 0:
                    pool.wait_ge(dn_psum, r)
                nc.gpsimd.tensor_tensor(hs[1][:, it], h[:, it % HB], hs[0][:, it].bitcast(F32), ALU.subtract).then_inc(
                    hl_ready, 1)

            def turn(g, first=False, last=False):
                for n in range(7):
                    scale_k(g, n)
                    if first and 2 <= n <= 5:
                        mix_add(1, n - 2)
                    elif not first and n >= 2:
                        h_low(g, n - 2)
                if first:
                    split_low(wu, wup, whi_ready, 1, wu_lo_ready)
                    split_low(wd, wdown, wd_hi_ready, 1, wd_lo_ready, 0, IT // 2)
                else:
                    h_low(g, 5)
                    h_low(g, 6)
                    if not last:
                        h_low(g, 7)
                group_rsqrt(g)
                if first:
                    mix_add(1, 4)
                    split_low(wg, wgate, whi_ready, 2, wg_lo_ready)
                elif last:
                    h_low(g, 7)
                else:
                    for i in range(5):
                        if i == 4:
                            rsqrt2(g)
                        mix_add(g + 1, i)
                rsqrt1(g)
                if first:
                    split_low(wd, wdown, wd_hi_ready, 2, wd_lo_ready, IT // 2, IT)
                if last:
                    rsqrt2(g)

            for i in range(5):
                mix_add(0, i)
            turn(0, first=True)
            with pool.Fori(1, G - 1) as g:
                turn(g)
            turn(G - 1, last=True)
            for it in range(IT):
                h_low(G, it)
            for j in range(J):
                rsqrt2(G + j)

        @block.scalar
        def _(act):
            act.dma_start(vec[:], d["vec"]).then_inc(L["vec"], 16)
            act.dma_start(w2[:], d["w2"]).then_inc(L["w2"], 16)
            act.dma_start(w2g[:], d["w2g"]).then_inc(L["w2"], 16)
            act.dma_start(dw2[:], d["dw2"]).then_inc(L["dw"], 16)

            def z(g):
                act.wait_ge(z_psum, g + 1)
                wait_last(act, mix_psum, 5 * g)
                nc.scalar.activation(zt[:], half(Z_BANK, 0), ACT.Tanh)
                nc.scalar.activation(ztg[:], bank[Z_BANK][0:DMIX, TG:2 * TG], ACT.Tanh).then_inc(z_tanh, 1)

            def decay_tanh(g):
                act.wait_ge(dec1_psum, g + 1)
                wait_last(act, dec2_psum, g)
                nc.scalar.activation(tdec[:], bank[DEC1_BANK][0:DDEC, 0:TG], ACT.Tanh).then_inc(dec1_tanh, 1)

            def k_out(g):
                act.wait_ge(k_psum, g + 1)
                wait_last(act, kT_psum, g)
                wait_last(act, k_scaled, 7 * g)
                nc.scalar.copy(kq[:], halves(PROJ_BANK["k"])).then_inc(k_ready, 1)

            def decay(g):
                act.wait_ge(dec2_psum, g + 1)
                wait_last(act, w_ready, g)
                for c in range(CH):
                    last = nc.scalar.activation(edec[:, c], half(DEC2_BANK, c), ACT.Exp, bias=vcol("decay", c))
                last.then_inc(exp_ready, 1)
                act.wait_ge(exp_ready, g + 1)
                wait_last(act, wprod, 7 * g)
                wait_last(act, k_scaled, 7 * g)
                nc.scalar.activation(wdec[0][:], edec[:], ACT.Exp, scale=-1.0).then_inc(w_ready, 1)

            def r_out(g):
                act.wait_ge(r_psum, g + 1)
                wait_last(act, q_scaled, 7 * g)
                wait_last(act, o_psum, 2 * g)
                for e in range(2):
                    lo, hi = e * HS, (e + 1) * HS
                    last = nc.scalar.copy(rq[lo:hi, :, e], halves(PROJ_BANK["r"])[lo:hi])
                last.then_inc(r_ready, 1)

            def v_out(g):
                act.wait_ge(v_psum, g + 1)
                wait_last(act, st_psum, 2 * g)
                nc.scalar.copy(vs[:], halves(PROJ_BANK["v"])).then_inc(v_ready, 1)

            def g_out(g):
                act.wait_ge(g_psum, g + 1)
                wait_last(act, og_ready, g)
                nc.scalar.activation(gT[:], halves(PROJ_BANK["g"]), ACT.Silu).then_inc(g_ready, 1)

            def bonus_out(g):
                act.wait_ge(bonus_psum, g + 1)
                wait_last(act, diag_written, g)
                nc.scalar.copy(bonus[:], bank[DIAG_BANK][:, 0:J * CH * 2].rearrange("p (a e) -> p a e", e=2)).then_inc(
                    bonus_copied, 1)

            def kT_out(g):
                act.wait_ge(kT_psum, g + 1)
                wait_last(act, st_psum, 2 * g)
                nc.scalar.copy(kT[:], bank[KT_BANK][:].rearrange("p (j c n) -> p j c n", j=J, c=CH)).then_inc(kT_ready, 1)

            def affine(g):
                act.wait_ge(nT_psum, g + 1)
                wait_last(act, og_ready, g)
                for c in range(CH):
                    last = nc.scalar.activation(nT[:, c], half(NT_BANK, c), ACT.Identity, bias=vcol("beta", c),
                                                scale=vcol("gamma", c))
                last.then_inc(nT_ready, 1)

            def y_signed(r):
                act.wait_ge(yT_psum, r + 1)
                act.wait_ge(yu_ready, r)
                nc.scalar.activation(ya[:], half(FFN_BANK, 0), ACT.Copy, scale=vcol("su_ug", 0)).then_inc(ya_ready, 1)

            def x_rotated(r):
                act.wait_ge(xh_psum, r + 1)
                act.wait_ge(ug_psum, IT * r)
                s = 1.0 / (C ** 0.5 * FFN_SCALE)
                nc.scalar.mul(xh[0][:, 0], half(FFN_BANK, 0), s)
                nc.scalar.mul(xh[0][:, 1], half(FFN_BANK, 1), -s).then_inc(xh_ready, 1)

            def silu(r, it):
                act.wait_ge(ug_psum, IT * r + it + 1)
                act.wait_ge(h_ready, IT * r + max(it - 1, 0))
                nc.scalar.activation(sg[:, it % 2], half(UG_BANK[it % 2], 1), ACT.Silu,
                                     scale=wsu[:, IT + it:IT + it + 1]).then_inc(silu_ready, 1)

            def split_high(name, parts, w):
                act.wait_ge(L[name], 16)
                nc.scalar.copy(parts[0][:], w[:]).then_inc(whi_ready, 1)

            def wd_high(pairs, lo, hi):
                act.wait_ge(wd_ready, pairs)
                nc.scalar.copy(wd[0][:, lo:hi], wdown[:, lo:hi]).then_inc(wd_hi_ready, 1)

            def h_high(r, it):
                act.wait_ge(h_ready, IT * r + it + 1)
                if it == 0:
                    act.wait_ge(dn_psum, r)
                nc.scalar.copy(hs[0][:, it], h[:, it % HB]).then_inc(hh_ready, 1)

            def silus(r, first=0, end=IT):
                for it in range(first, end):
                    silu(r, it)
                    if it > first:
                        h_high(r, it - 1)
                h_high(r, end - 1)

            def turn(g, first=False, last=False):
                if first:
                    bonus_out(0)
                    z(1)
                    split_high("wup", wu, wup)
                    split_high("wgate", wg, wgate)
                else:
                    x_rotated(g)
                    bonus_out(g)
                    silus(g, 0, 5 if last else IT)
                    if last:
                        silus(g, 5, 6)
                kT_out(g)
                if first:
                    decay_tanh(1)
                    wd_high(2, 0, IT // 2)
                    k_out(1)
                    affine(0)
                    decay(1)
                    r_out(1)
                    v_out(1)
                    wd_high(4, IT // 2, IT)
                    y_signed(1)
                    g_out(1)
                elif last:
                    silus(g, 6, 7)
                    silus(g, 7, IT)
                    affine(g)
                    y_signed(g + 1)
                else:
                    z(g + 1)
                    affine(g)
                    decay_tanh(g + 1)
                    k_out(g + 1)
                    decay(g + 1)
                    r_out(g + 1)
                    v_out(g + 1)
                    y_signed(g + 1)
                    g_out(g + 1)

            act.wait_ge(zeroed, 1)
            nc.scalar.activation(zt[:], rq[:, 0, 0], ACT.Tanh).then_inc(tanh_loaded, 1)
            act.wait_ge(L["vec"], 16)
            act.wait_ge(tanh_loaded, 1)
            z(0)
            decay_tanh(0)
            k_out(0)
            decay(0)
            r_out(0)
            v_out(0)
            g_out(0)
            turn(0, first=True)
            act.wait_ge(scales_ready, 1)
            with act.Fori(1, G - 1) as g:
                turn(g)
            turn(G - 1, last=True)
            x_rotated(G)
            silus(G)

        @block.vector
        def _(dve):
            def token_mix(g):
                dve.wait_ge(xT_loaded, 16 * g + 16)
                nc.vector.tensor_tensor(xx[:], before, now, ALU.subtract).then_inc(xx_done, 1)
                dve.wait_ge(xx_done, g + 1)
                if isinstance(g, int) and g == 0:
                    dve.wait_ge(L["vec"], 16)
                wait_last(dve, z_psum, g)
                for c in range(CH):
                    last = nc.vector.scalar_tensor_tensor(xxx[:, c], xx[:, c], vcol("maa_x", c), now[:, c],
                                                          ALU.mult, ALU.add)
                last.then_inc(xxx_ready, 1)

            def mix(g, i):
                dve.wait_ge(mix_psum, 5 * g + i + 1)
                wait_last(dve, xm_ready, 5 * g + max(i - 1, 0))
                for c in range(CH):
                    last = nc.vector.scalar_tensor_tensor(mixed[:, i % 2, c], half(MIX_BANK[MIXES[i]], c),
                                                          vcol("maa_" + MIXES[i], c), xx[:, c], ALU.add, ALU.mult)
                last.then_inc(mixed_ready, 1)

            def r_u_k(g):
                dve.wait_ge(r_ready, g + 1)
                dve.wait_ge(k_ready, g + 1)
                wait_last(dve, bonus_psum, g)
                for c in range(CH):
                    last = nc.vector.scalar_tensor_tensor(ruk[:, c], half(PROJ_BANK["r"], c), vcol("u", c), kq[:, c],
                                                          ALU.mult, ALU.mult)
                last.then_inc(ruk_ready, 1)

            def diagonal(g):
                dve.wait_ge(bonus_copied, g + 1)
                wait_last(dve, o_psum, 2 * g)
                n = J * CH * 2
                nc.vector.tensor_tensor(A[:].rearrange("p a e t -> p (a e) t"),
                                        ident.rearrange("p (a t) -> p a t", a=1).to_broadcast([P, n, Q]),
                                        bonus[:].rearrange("p a (e t) -> p (a e) t", t=1).to_broadcast([P, n, Q]),
                                        ALU.mult).then_inc(diag_written, 1)

            def level(g, n, between=None):
                Ln = LEVELS[n]
                nb = TG // (2 * Ln)
                dve.wait_ge(level_psum, 7 * g + n + 1)
                if n == 0:
                    dve.wait_ge(w_ready, g + 1)
                else:
                    dve.wait_ge(wprod, 7 * g + n)
                    dve.wait_ge(q_scaled, 7 * g + n)
                w4 = wdec[n][:].rearrange("p c (b e) -> p c b e", e=2)
                for e in range(2):
                    lo, hi = e * HS, (e + 1) * HS
                    qq = rq[lo:hi, :, e].rearrange("p c (b e l) -> p c b e l", e=2, l=Ln)[:, :, :, 1]
                    last = nc.vector.tensor_tensor(qq, qq, w4[lo:hi, :, :, 0:1].to_broadcast([HS, CH, nb, Ln]), ALU.mult)
                last.then_inc(q_scaled, 1)
                if n == 0:
                    diagonal(g)
                    dve.wait_ge(diag_written, g + 1)
                else:
                    dve.wait_ge(A_copied, 7 * g + n)
                nc.vector.tensor_tensor(wdec[n + 1][:], w4[:, :, :, 0], w4[:, :, :, 1], ALU.mult).then_inc(wprod, 1)
                if between is not None:
                    between()
                m0 = HALF * n
                nbq = Q // (2 * Ln)
                m = J * CH * 2
                nc.vector.copy_predicated(
                    A[:].rearrange("p a e (b h l) -> p (a e) b h l", h=2, l=Ln)[:, :, :, 1],
                    masks[:, m0:m0 + HALF].bitcast(U32).rearrange("p (a b l) -> p a b l", a=1, l=Ln).to_broadcast(
                        [P, m, nbq, Ln]),
                    bank[LEVEL_BANK[n % 2]][:].rearrange("p (a b l) -> p a b l", a=m, l=Ln)).then_inc(A_copied, 1)

            def state(g, j):
                dve.wait_ge(st_psum, 2 * g + j + 1)
                dve.wait_ge(o_psum, 2 * g + j + 1)
                wait_last(dve, S_ready, 2 * g + j)
                dve.wait_ge(wprod, 7 * g + 7)
                for c in range(CH):
                    for e in range(2):
                        lo, hi = e * HS, (e + 1) * HS
                        last = nc.vector.scalar_tensor_tensor(
                            S[lo:hi, c, lo:hi], S[lo:hi, c, lo:hi], wdec[7][lo:hi, c, j:j + 1],
                            bank[STATE_BANK[j]][lo:hi, c * P + lo:c * P + hi], ALU.mult, ALU.add)
                last.then_inc(S_ready, 1)

            def moments(g, stat, m, n, eps, parts_done, var_ready):
                nc.vector.tensor_tensor(m["diff"][:], stat[:, :, 1], stat[:, :, 4], ALU.subtract)
                nc.vector.tensor_tensor(m["m2"][:], stat[:, :, 2], stat[:, :, 5], ALU.add)
                nc.vector.tensor_tensor(m["sum"][:], stat[:, :, 1], stat[:, :, 4], ALU.add).then_inc(parts_done, 1)
                dve.wait_ge(parts_done, 3 * g + 1)
                nc.vector.scalar_tensor_tensor(m["sq"][:], m["diff"][:], 0.25, m["diff"][:], ALU.mult, ALU.mult)
                nc.vector.tensor_scalar(m["m2n"][:], m["m2"][:], 1.0 / n, eps, ALU.mult,
                                        ALU.add).then_inc(parts_done, 1)
                dve.wait_ge(parts_done, 3 * g + 2)
                nc.vector.tensor_tensor(m["var"][:], m["sq"][:], m["m2n"][:], ALU.add).then_inc(var_ready, 1)
                nc.vector.tensor_scalar(m["mean"][:], m["sum"][:], 0.5, None, ALU.mult).then_inc(parts_done, 1)

            heads_out = bank[OUT_BANK][:].rearrange("p (a n) -> p a n", n=HS)

            def per_head(t):
                return t[:].rearrange("p j (h n) -> p (j h) n", n=HS)

            def of_head(t):
                return t[:].rearrange("p (a n) -> p a n", n=1).to_broadcast([P, J * HEADS, HS])

            def group_norm(g):
                dve.wait_ge(o_psum, 2 * g + 2)
                for j in range(J):
                    for hh in range(HEADS):
                        last = nc.vector.bn_stats(gstat[:, j * HEADS + hh],
                                                  bank[OUT_BANK][:, j * C + hh * HS:j * C + (hh + 1) * HS])
                last.then_inc(gstat_done, 1)
                dve.wait_ge(gstat_done, g + 1)
                wait_last(dve, grs_ready, g)
                moments(g, gstat, gm, HS, GN_EPS, gmv_done, gvar_ready)
                dve.wait_ge(gmv_done, 3 * g + 3)
                wait_last(dve, nT_psum, g)
                nc.vector.tensor_tensor(per_head(norm), heads_out, of_head(gm["mean"]), ALU.subtract).then_inc(centred, 1)

            def group_norm_apply(g):
                dve.wait_ge(centred, g + 1)
                dve.wait_ge(grs_ready, g + 1)
                nc.vector.tensor_tensor(per_head(norm), per_head(norm), of_head(grs), ALU.mult).then_inc(norm_ready, 1)

            def gate(g):
                dve.wait_ge(nT_ready, g + 1)
                dve.wait_ge(g_ready, g + 1)
                wait_last(dve, wo_psum, g)
                nc.vector.tensor_tensor(og[:], nT[:], gT[:], ALU.mult).then_inc(og_ready, 1)

            def residual1(g):
                dve.wait_ge(wo_psum, g + 1)
                wait_last(dve, y_ready, g)
                dve.wait_ge(xtok_loaded, 16 * g + 16)
                nc.vector.tensor_tensor(res[:], halves(WO_BANK), xtok[:], ALU.add).then_inc(res_ready, 1)
                dve.wait_ge(res_ready, g)
                moments1(g, res[:])

            def moments1(g, a):
                dve.wait_ge(wo_psum, g + 1)
                for j in range(J):
                    last = nc.vector.bn_stats(stat1[:, j], a[:, j])
                last.then_inc(stat1_done, 1)
                dve.wait_ge(stat1_done, g + 1)
                moments(g, stat1, m1, C, LN_EPS, mv1_done, var1_ready)

            def norm1(g, a):
                dve.wait_ge(rs1_ready, g + 1)
                dve.wait_ge(mv1_done, 3 * g + 3)
                dve.wait_ge(yT_psum, g + 1)
                dve.wait_ge(res2_ready, g + 1)
                for j in range(J):
                    last = nc.vector.tensor_scalar(y[:, j], a[:, j], m1["mean"][:, j:j + 1], rs1[:, j:j + 1], ALU.subtract,
                                                   ALU.mult)
                last.then_inc(y_ready, 1)

            def rotate_down(s):
                a, o = ((wdownT, wdown), (wdown, wdownT))[s]
                if s == 0:
                    dve.wait_ge(L["wdown"], 16)
                else:
                    dve.wait_ge(wd_step, 1)
                a, o = (t[:].rearrange("p (b e l) c -> p b e (l c)", e=2, l=2 - s) for t in (a, o))
                nc.vector.tensor_tensor(o[:, :, 0], a[:, :, 0], a[:, :, 1], ALU.add)
                nc.vector.tensor_tensor(o[:, :, 1], a[:, :, 0], a[:, :, 1], ALU.subtract).then_inc(wd_step, 1)

            def scale_down(i):
                if i == 0:
                    dve.wait_ge(L["wsrow"], 16)
                    dve.wait_ge(wd_step, 2)
                dve.wait_ge(wd_psum, i + 1)
                for e in range(2):
                    it = 2 * i + e
                    last = nc.vector.scalar_tensor_tensor(wdown[:, it], half(WD_BANK[i // 2], e), sdu[:, it:it + 1], wsrow[:],
                                                          ALU.mult, ALU.mult)
                last.then_inc(wd_ready, 1)

            def y_butterfly(r):
                dve.wait_ge(ya_ready, r + 1)
                dve.wait_ge(xh_psum, r)
                nc.vector.scalar_tensor_tensor(yu[:, 0], half(FFN_BANK, 1), vcol("su_ug", 1), ya[:], ALU.mult, ALU.add)
                nc.vector.scalar_tensor_tensor(yu[:, 1], half(FFN_BANK, 1), vcol("su_ug", 1), ya[:], ALU.mult,
                                               ALU.subtract).then_inc(yu_ready, 1)

            def x_low(r):
                dve.wait_ge(xh_ready, r + 1)
                dve.wait_ge(ug_psum, IT * r)
                s = 1.0 / (C ** 0.5 * FFN_SCALE)
                for c in range(CH):
                    last = nc.vector.scalar_tensor_tensor(xh[1][:, c], half(FFN_BANK, c), -s if c else s,
                                                          xh[0][:, c].bitcast(F32), ALU.mult, ALU.subtract)
                last.then_inc(xl_ready, 1)

            def swiglu(r, it):
                dve.wait_ge(silu_ready, IT * r + it + 1)
                dve.wait_ge(hl_ready, IT * r + it + 1 - HB)
                nc.vector.scalar_tensor_tensor(h[:, it % HB], half(UG_BANK[it % 2], 0), wsu[:, it:it + 1], sg[:, it % 2],
                                               ALU.mult, ALU.mult).then_inc(h_ready, 1)

            def residual2(r):
                dve.wait_ge(dn_psum, r + 1)
                dve.wait_ge(out_ready, r)
                dve.wait_ge(y_ready, r)
                nc.vector.tensor_tensor(res2[:], halves(FFN_BANK), y[:], ALU.add).then_inc(res2_ready, 1)

            def moments2(r, a, added, j0=0, j1=J):
                dve.wait_ge(added, r + 1)
                for j in range(j0, j1):
                    last = nc.vector.bn_stats(stat2[:, j], a[:, j])
                last.then_inc(stat2_done, 1)
                dve.wait_ge(stat2_done, r)
                moments(r - 1, stat2, m2, C, LN_EPS, mv2_done, var2_ready)

            def norm2(r, a, j0=0, j1=J):
                dve.wait_ge(rs2_ready, r + 1)
                dve.wait_ge(mv2_done, 3 * r)
                dve.wait_ge(stored, 16 * min(r, G) if isinstance(r, int) else 16 * r)
                for j in range(j0, j1):
                    last = nc.vector.tensor_scalar(outs[:, j], a[:, j], m2["mean"][:, j:j + 1], rs2[:, j:j + 1],
                                                   ALU.subtract, ALU.mult)
                last.then_inc(out_ready, 1)

            def turn(g, first=False, last=False):
                if not first:
                    x_low(g)
                for n in range(7):
                    level(g, n, (lambda: swiglu(g, n - 1)) if not first and 1 <= n <= (5 if last else 6) else None)
                    if first:
                        if 1 <= n <= 4:
                            mix(1, n - 1)
                        if n in DOWN_AT:
                            scale_down(DOWN_AT.index(n))
                if last:
                    swiglu(g, 5)
                elif not first:
                    swiglu(g, 6)
                    swiglu(g, 7)
                state(g, 0)
                if first:
                    scale_down(2)
                elif last:
                    swiglu(g, 6)
                else:
                    token_mix(g + 1)
                group_norm(g)
                if last:
                    swiglu(g, 7)
                else:
                    state(g, 1)
                    if not first:
                        mix(g + 1, 0)
                group_norm_apply(g)
                if first:
                    mix(1, 4)
                    gate(0)
                elif last:
                    gate(g)
                else:
                    mix(g + 1, 1)
                    residual2(g)
                    mix(g + 1, 2)
                    gate(g)
                    mix(g + 1, 3)
                    moments2(g, res2, res2_ready)
                    mix(g + 1, 4)
                    norm2(g, res2)
                if first or last:
                    moments1(g, halves(WO_BANK))
                    if last:
                        residual2(g)
                    norm1(g, halves(WO_BANK))
                    if first:
                        scale_down(3)
                else:
                    residual1(g)
                    norm1(g, res[:])
                if not last:
                    r_u_k(g + 1)
                y_butterfly(g + 1)

            dve.wait_ge(zeroed, 1)
            token_mix(0)
            nc.vector.tensor_scalar(wsu[:], vec[:, VEC["ws_up"]:VEC["ws_up"] + 2 * IT], FFN_SCALE, None, ALU.mult)
            nc.vector.tensor_scalar(sdu[:], vec[:, VEC["su_dp"]:VEC["su_dp"] + IT],
                                    1.0 / INTER ** 0.5, None, ALU.mult).then_inc(scales_ready, 1)
            dve.wait_ge(scales_ready, 1)
            for i in range(5):
                mix(0, i)
            rotate_down(0)
            rotate_down(1)
            r_u_k(0)
            token_mix(1)
            dve.wait_ge(L["const"], 16)
            turn(0, first=True)
            with dve.Fori(1, G - 1) as g:
                turn(g)
            turn(G - 1, last=True)
            x_low(G)
            moments2(G - 1, res2, res2_ready)
            for it in range(IT):
                swiglu(G, it)
                if it == 1:
                    norm2(G - 1, res2)
            for j in range(J):
                moments2(G + j, halves(LAST_BANK[j]), dn_psum, j, j + 1)
                norm2(G + j, halves(LAST_BANK[j]), j, j + 1)

        @block.tensor
        def _(pe):
            def loaded(name, count=16):
                pe.wait_ge(L[name], count)

            def keep_warm(n, a=flat(xm["w"])):
                for _ in range(n):
                    nc.tensor.matmul(bank[LEVEL_BANK[0]][:, 0:TG], a[:, 0:P], a[:, 0:TG], start=True, stop=True)

            def z(g):
                pe.wait_ge(xxx_ready, g + 1)
                if isinstance(g, int) and g == 1:
                    pe.wait_ge(v_ready, 1)
                elif not isinstance(g, int):
                    pe.wait_ge(h_ready, IT * g)
                for c in range(CH):
                    nc.tensor.matmul(half(Z_BANK, 0), w1[:, c, 0:P], xxx[:, c], start=c == 0, stop=c == CH - 1)
                for c in range(CH):
                    last = nc.tensor.matmul(bank[Z_BANK][0:DMIX, TG:2 * TG], w1[:, c, P:P + DMIX], xxx[:, c],
                                            start=c == 0, stop=c == CH - 1)
                last.then_inc(z_psum, 1)

            def mix(g, i, early=False):
                n = MIXES[i]
                f = PART[n]
                if i == 0:
                    pe.wait_ge(z_tanh, g + 1)
                    if early:
                        pe.wait_ge(g_ready, 1)
                elif n == "k" and not early:
                    wait_last(pe, kT_ready, g)
                elif n == "r":
                    if early:
                        pe.wait_ge(bonus_copied, 1)
                    else:
                        wait_last(pe, S_ready, 2 * g)
                elif n == "v":
                    wait_last(pe, res2_ready, g)
                lo, hi = (0, DMIX) if n == "g" else (f * DMIX, (f + 1) * DMIX)
                for c in range(CH):
                    w, zz = (w2g, ztg) if n == "g" else (w2, zt)
                    last = nc.tensor.matmul(half(MIX_BANK[n], c), w[lo:hi, c * P:(c + 1) * P], zz[lo:hi, :], start=True,
                                            stop=True, tile_position=(lo, 0))
                last.then_inc(mix_psum, 1)

            def dec1(g):
                pe.wait_ge(xm_ready, 5 * g + 1)
                for c in range(CH):
                    last = nc.tensor.matmul(bank[DEC1_BANK][0:DDEC, 0:TG], dw1[:, c], xm["w"][:, c], start=c == 0,
                                            stop=c == CH - 1)
                last.then_inc(dec1_psum, 1)

            def dec2(g):
                pe.wait_ge(dec1_tanh, g + 1)
                pe.wait_ge(mixed_ready, 5 * g + 3)
                for c in range(CH):
                    last = nc.tensor.matmul(half(DEC2_BANK, c), dw2[:, c * P:(c + 1) * P], tdec[:], start=True, stop=True)
                last.then_inc(dec2_psum, 1)

            def channels(g, n, done):
                i = MIXES.index(n)
                pe.wait_ge(xm_ready, 5 * g + i + 1)
                if n == "r":
                    wait_last(pe, S_ready, 2 * g)
                for a in range(CH):
                    for c in range(CH):
                        last = nc.tensor.matmul(half(PROJ_BANK[n], a), proj[n][:, c, a * P:(a + 1) * P], xm[n][:, c],
                                                start=c == 0, stop=c == CH - 1)
                last.then_inc(done, 1)

            def v(g):
                pe.wait_ge(xm_ready, 5 * g + 4)
                pe.wait_ge(mixed_ready, 5 * g + 5)
                for j in range(J):
                    for c in range(CH):
                        last = nc.tensor.matmul(half(PROJ_BANK["v"], j), xm["v"][:, c, j * Q:(j + 1) * Q],
                                                proj["v"][:, c], start=c == 0, stop=c == CH - 1)
                last.then_inc(v_psum, 1)

            def diagonal(g):
                pe.wait_ge(ruk_ready, g + 1)
                pe.wait_ge(w_ready, g + 1)
                for a in range(J * CH):
                    j, c = divmod(a, CH)
                    last = nc.tensor.matmul(bank[DIAG_BANK][:, 2 * a:2 * a + 2], ruk[:, c, j * Q:(j + 1) * Q], heads,
                                            start=True, stop=True)
                last.then_inc(bonus_psum, 1)

            def level(g, n):
                Ln = LEVELS[n]
                if n == 0:
                    pe.wait_ge(k_ready, g + 1)
                    pe.wait_ge(r_ready, g + 1)
                    wait_last(pe, nT_ready, g)
                elif n == 1:
                    pe.wait_ge(q_scaled, 7 * g + 1)
                    pe.wait_ge(k_scaled, 7 * g + 1)
                    pe.wait_ge(ruk_ready, g + 1)
                else:
                    pe.wait_ge(q_scaled, 7 * g + n)
                    pe.wait_ge(k_scaled, 7 * g + n)
                    pe.wait_ge(A_copied, 7 * g + n - 1)
                for a in range(J * CH):
                    j, c = divmod(a, CH)
                    qq = rq[:, c, :, j * Q:(j + 1) * Q].rearrange("p e (b h l) -> p e b h l", h=2, l=Ln)[:, :, :, 1]
                    last = nc.tensor.matmul(
                        bank[LEVEL_BANK[n % 2]][:, a * Q:(a + 1) * Q].rearrange("p (e b l) -> p e b l", e=2, l=Ln),
                        kq[:, c, j * Q:(j + 1) * Q], qq, start=True, stop=True)
                last.then_inc(level_psum, 1)

            def k_transpose(g, first):
                pe.wait_ge(k_scaled, 7 * g + 7)
                if first:
                    pe.wait_ge(mixed_ready, 5 + 2)
                for a in range(J * CH):
                    j, c = divmod(a, CH)
                    last = nc.tensor.transpose(bank[KT_BANK][:, a * P:(a + 1) * P], kq[:, c, j * Q:(j + 1) * Q], ident)
                last.then_inc(kT_psum, 1)

            def chunk(g, j, first):
                if j == 0:
                    if first:
                        pe.wait_ge(wd_ready, 2)
                    pe.wait_ge(A_copied, 7 * g + 7)
                    pe.wait_ge(q_scaled, 7 * g + 7)
                    pe.wait_ge(v_ready, g + 1)
                    wait_last(pe, y_ready, g)
                wait_last(pe, S_ready, 2 * g + j)
                for c in range(CH):
                    at = j * C + c * P
                    for e in range(2):
                        nc.tensor.matmul(bank[OUT_BANK][:, at + e * HS:at + (e + 1) * HS], rq[:, c, e, j * Q:(j + 1) * Q],
                                         S[:, c, e * HS:(e + 1) * HS], start=True, stop=False)
                        last = nc.tensor.matmul(bank[OUT_BANK][:, at + e * HS:at + (e + 1) * HS], A[:, j * CH + c, e],
                                                vs[:, j, c * P + e * HS:c * P + (e + 1) * HS], start=False, stop=True)
                last.then_inc(o_psum, 1)
                if j == 0:
                    pe.wait_ge(kT_ready, g + 1)
                    pe.wait_ge(bonus_copied, g + 1)
                    if first:
                        pe.wait_ge(mixed_ready, 5 + 3)
                for c in range(CH):
                    last = nc.tensor.matmul(bank[STATE_BANK[j]][:, c * P:(c + 1) * P], kT[:, j, c],
                                            vs[:, j, c * P:(c + 1) * P], start=True, stop=True)
                last.then_inc(st_psum, 1)

            def norm_transpose(g):
                pe.wait_ge(norm_ready, g + 1)
                for c in range(CH):
                    for j in range(J):
                        last = nc.tensor.transpose(bank[NT_BANK][:, c * TG + j * Q:c * TG + (j + 1) * Q],
                                                   norm[:, j, c * P:(c + 1) * P], ident)
                last.then_inc(nT_psum, 1)

            def w_o(g, add_x=False):
                if add_x:
                    pe.wait_ge(norm_ready, g + 1)
                    pe.wait_ge(xtok_loaded, 16 * g + 16)
                    nc.tensor.matmul(bank[WO_BANK][:], ident, flat(xtok), start=True, stop=False)
                pe.wait_ge(og_ready, g + 1)
                for j in range(J):
                    for c in range(CH):
                        last = nc.tensor.matmul(half(WO_BANK, j), og[:, c, j * Q:(j + 1) * Q], proj["o"][:, c],
                                                start=c == 0 and not add_x,
                                                stop=c == CH - 1 and (j == J - 1 or not add_x))
                last.then_inc(wo_psum, 1)

            def rotate_down(i):
                if i == 0:
                    pe.wait_ge(wd_step, 2)
                else:
                    pe.wait_ge(wd_ready, i)
                if i == 2:
                    pe.wait_ge(mixed_ready, 5 + 4)
                for e, m in enumerate((had, had_neg if i >= 2 else had)):
                    t = 4 * e + 2 * (i % 2)
                    last = nc.tensor.matmul(bank[WD_BANK[i // 2]][:], m, wdownT[:, t:t + 2].rearrange("p a c -> p (a c)"),
                                            start=e == 0, stop=e == 1)
                last.then_inc(wd_psum, 1)

            def y_transpose(r, first=False, last=False):
                pe.wait_ge(y_ready, r)
                if first:
                    pe.wait_ge(wd_ready, IT // 2)
                elif not last:
                    pe.wait_ge(mixed_ready, 5 * r + 4)
                pe.wait_ge(res2_ready, r)
                for c in range(CH):
                    for j in range(J):
                        last = nc.tensor.transpose(bank[FFN_BANK][:, c * TG + j * Q:c * TG + (j + 1) * Q],
                                                   y[:, j, c * P:(c + 1) * P], ident)
                last.then_inc(yT_psum, 1)

            def rotate_x(r):
                pe.wait_ge(yu_ready, r + 1)
                nc.tensor.matmul(bank[FFN_BANK][:], had, yu[:].rearrange("p c t -> p (c t)"), start=True,
                                 stop=True).then_inc(xh_psum, 1)

            def up_gate(r, it):
                if it == 0:
                    pe.wait_ge(xl_ready, r + 1)
                if it <= 1 and (not isinstance(r, int) or r < G):
                    pe.wait_ge((v_ready, g_ready)[it], r + 1)
                pe.wait_ge(h_ready, IT * r + max(it - 1, 0))
                b = UG_BANK[it % 2]
                for e, w in enumerate((wu, wg)):
                    terms = [(c, wp, xp) for c in range(CH) for wp, xp in ((1, 0), (0, 1), (0, 0))]
                    for n, (c, wp, xp) in enumerate(terms):
                        last = nc.tensor.matmul(half(b, e), w[wp][:, c, it * P:(it + 1) * P], xh[xp][:, c], start=n == 0,
                                                stop=n == len(terms) - 1)
                last.then_inc(ug_psum, 1)

            def down(r, j, first=0, end=IT, b=FFN_BANK, add_y=False):
                if add_y:
                    nc.tensor.matmul(half(b, j), ident, y[:, j], start=True, stop=False)
                for it in range(first, end):
                    if j == 0:
                        pe.wait_ge(hl_ready, IT * r + it + 1)
                    for hp, wp in ((1, 0), (0, 1), (0, 0)):
                        last = nc.tensor.matmul(half(b, j), hs[hp][:, it, j * Q:(j + 1) * Q], wd[wp][:, it],
                                                start=it == 0 and hp == 1 and not add_y,
                                                stop=it == IT - 1 and hp == wp == 0)
                if end == IT and (j == J - 1 or add_y):
                    last.then_inc(dn_psum, 1)

            def turn(g, first=False, last=False):
                if not first:
                    rotate_x(g)
                diagonal(g)
                for n in range(7):
                    level(g, n)
                    if first:
                        if n == 0:
                            z(1)
                        elif n <= 4:
                            mix(1, n - 1, early=True)
                        elif n == 6:
                            dec1(1)
                        if n in DOWN_AT:
                            rotate_down(DOWN_AT.index(n))
                    elif not last or n <= 4:
                        up_gate(g, n)
                    elif n == 6:
                        up_gate(g, 5)
                if not first and not last:
                    up_gate(g, 7)
                k_transpose(g, first)
                chunk(g, 0, first)
                if first:
                    rotate_down(2)
                    chunk(0, 1, first)
                    channels(1, "k", k_psum)
                    dec2(1)
                    mix(1, 4, early=True)
                    norm_transpose(0)
                    channels(1, "r", r_psum)
                    loaded("W_o")
                    w_o(0, add_x=True)
                    v(1)
                    rotate_down(3)
                    channels(1, "g", g_psum)
                    y_transpose(1, first=True)
                    keep_warm(3)
                elif last:
                    up_gate(g, 6)
                    chunk(g, 1, first)
                    up_gate(g, 7)
                    down(g, 0, 0, 7)
                    norm_transpose(g)
                    down(g, 0, 7)
                    down(g, 1, 0, 3)
                    w_o(g, add_x=True)
                    down(g, 1, 3)
                    keep_warm(4)
                    y_transpose(G, last=True)
                    keep_warm(3)
                else:
                    down(g, 0)
                    chunk(g, 1, first)
                    z(g + 1)
                    down(g, 1, 0, 3)
                    mix(g + 1, 0)
                    down(g, 1, 3, 5)
                    mix(g + 1, 1)
                    down(g, 1, 5)
                    norm_transpose(g)
                    for i in range(2, 5):
                        mix(g + 1, i)
                    dec1(g + 1)
                    channels(g + 1, "k", k_psum)
                    w_o(g)
                    dec2(g + 1)
                    channels(g + 1, "r", r_psum)
                    v(g + 1)
                    y_transpose(g + 1)
                    channels(g + 1, "g", g_psum)

            pe.wait_ge(warm_operand, 1)
            keep_warm(5)
            loaded("w1")
            z(0)
            keep_warm(2)
            loaded("w2", 32)
            for i in range(3):
                mix(0, i)
            keep_warm(2, flat(w1))
            loaded("dw", 32)
            dec1(0)
            mix(0, 3)
            mix(0, 4)
            loaded("W_k")
            channels(0, "k", k_psum)
            dec2(0)
            loaded("W_r")
            channels(0, "r", r_psum)
            loaded("W_v")
            v(0)
            loaded("W_g")
            channels(0, "g", g_psum)
            loaded("const")
            turn(0, first=True)
            pe.wait_ge(wu_lo_ready, 1)
            pe.wait_ge(wg_lo_ready, 1)
            pe.wait_ge(wd_lo_ready, 2)
            with pe.Fori(1, G - 1) as g:
                turn(g)
            turn(G - 1, last=True)
            rotate_x(G)
            keep_warm(3)
            for it in range(IT):
                up_gate(G, it)
            for j in range(J):
                down(G, j, b=LAST_BANK[j], add_y=True)


def _masks(np):
    s = np.arange(Q)[:, None]
    parts = []
    for n in LEVELS:
        t = np.arange(Q)
        t = t[(t // n) % 2 == 1][None, :]
        parts.append((s // (2 * n) == t // (2 * n)) & ((s // n) % 2 == 0))
    return np.concatenate(parts, axis=1).astype(np.float32)


def _hadamard(np):
    m = np.ones((1, 1), np.float32)
    while m.shape[0] < P:
        m = np.block([[m, m], [m, -m]])
    return m


def kernel(**inputs):
    import numpy as np
    import concourse.bacc as _bacc
    from concourse import mybir as _mybir
    from concourse.bass_utils import run_bass_kernel_spmd as _run

    a = {k: np.asarray(v) for k, v in inputs.items()}
    A_, F_ = "L0_attn_", "L0_ffn_"

    def rows(m):
        return m.reshape(-1, P, m.shape[1]).transpose(1, 0, 2)

    def cols(v):
        return v.reshape(-1, P).T

    x = a[A_ + "hidden"][0]
    had = _hadamard(np)
    w2 = a[A_ + "time_maa_w2"]
    vec = [cols(a[A_ + "time_maa_" + n]) for n in "xwkrvg"]
    vec += [cols(a[A_ + n]) for n in ("time_decay", "time_faaaa", "ln_gamma", "ln_beta")]
    vec += [cols(a[F_ + n]) for n in ("SU_ug", "Wscale_ug", "SU_dp")]
    arrays = {
        "xT": rows(x.T), "xtok": rows(x), "vec": np.concatenate(vec, axis=1),
        "w1": rows(a[A_ + "time_maa_w1"]), "w2": w2[0:4].reshape(P, C), "w2g": w2[4],
        "dw1": rows(a[A_ + "time_decay_w1"]), "dw2": a[A_ + "time_decay_w2"],
        "wup": rows(a[F_ + "W_up"].T), "wgate": rows(a[F_ + "W_gate"].T), "wdown": rows(a[F_ + "W_down"].T),
        "wsrow": a[F_ + "Wscale_dp"].reshape(1, C),
        "const": np.concatenate([had, -had, np.eye(P, dtype=np.float32),
                                 np.kron(np.eye(2, dtype=np.float32), np.ones((HS, 1), np.float32)), _masks(np)], axis=1),
    }
    for n in "krvgo":
        arrays["W_" + n] = rows(a[A_ + "W_" + n].T)
    arrays = {k: np.ascontiguousarray(v) for k, v in arrays.items()}

    nc = _bacc.Bacc("TRN2", target_bir_lowering=False, num_devices=1)
    d = {k: nc.dram_tensor(f"{k}_dram", v.shape, _mybir.dt.from_np(v.dtype), kind="ExternalInput").ap()
         for k, v in arrays.items()}
    out = nc.dram_tensor("out_dram", (1, T, C), F32, kind="ExternalOutput").ap()
    d["out"] = out.rearrange("o (j p) c -> p (o j) c", p=P)
    build(nc, d)
    r = _run(nc, [{f"{k}_dram": v for k, v in arrays.items()}], core_ids=[0])
    return r.results[0]["out_dram"]
```
